# Optimizing a Trainium2 kernel written in Bass

```python
import numpy as np
import jax
import jax.numpy as jnp

def _softmax(x, axis=-1):
    return jax.nn.softmax(x, axis=axis)

def _gelu(x):
    return jax.nn.gelu(x, approximate=True)

def _silu(x):
    return jax.nn.silu(x)

def _sigmoid(x):
    return jax.nn.sigmoid(x)

def _layernorm(x, axis=-1, eps=1e-05):
    m = jnp.mean(x, axis=axis, keepdims=True)
    v = jnp.var(x, axis=axis, keepdims=True)
    return (x - m) / jnp.sqrt(v + eps)

def _scatter_add(tgt, idx, src, axis=0):
    return tgt.at[idx].add(src)

def _segment_sum(src, seg, n):
    return jax.ops.segment_sum(src, seg, n)
kernel_name = 'mk_seq_postln_d1_jaxref_r4_8657d5'

def setup_inputs(seed: int=0):
    np.random.seed(seed)
    _w = jnp.asarray

    def _L0_attn_setup():
        import jax, jax.numpy as jnp
        import numpy as np
        H = 16
        EPS_DEN = 1e-06

        def _decay_scan(x, decay, init):
            xT = jnp.moveaxis(x, 2, 0)

            def step(s, xt):
                s = decay * s + xt
                return (s, s)
            _, ys = jax.lax.scan(step, init, xT)
            return jnp.moveaxis(ys, 0, 2)

        def _phi(z):
            return jax.nn.elu(z) + 1.0

        def _reference_tuple_inner(x, w_qkv, w_out, decay_param):
            B, T, Hid = x.shape
            D = Hid // H
            qkv = x @ w_qkv
            q, k, v = jnp.split(qkv, 3, axis=-1)

            def to_bhtd(t):
                return t.reshape(B, T, H, D).transpose(0, 2, 1, 3)
            q = _phi(to_bhtd(q))
            k = _phi(to_bhtd(k))
            v = to_bhtd(v)
            decay = jax.nn.sigmoid(decay_param).reshape(1, H, 1)
            init = jnp.zeros((B, H, D), dtype=x.dtype)
            running_kv = _decay_scan(k * v, decay, init)
            running_ksum = _decay_scan(k, decay, init)
            den = jnp.clip(jnp.sum(q * running_ksum, axis=-1, keepdims=True), EPS_DEN, None)
            out = q * running_kv / den
            out = out.transpose(0, 2, 1, 3).reshape(B, T, Hid) @ w_out
            new_kv = running_kv[:, :, -1, :]
            new_ksum = running_ksum[:, :, -1, :]
            return (out, new_kv, new_ksum)
        key = jax.random.key(seed)
        k1, k2, k3 = jax.random.split(key, 3)
        x = jax.random.normal(k1, (2, 1024, 512), dtype=jnp.float32)
        w_qkv = jax.random.normal(k2, (512, 1536), dtype=jnp.float32) * 0.02
        w_out = jax.random.normal(k3, (512, 512), dtype=jnp.float32) * 0.02
        decay_param = jnp.full((H,), 0.95, dtype=jnp.float32)
        return {'x': x, 'w_qkv': w_qkv, 'w_out': w_out, 'decay_param': decay_param}
    _L0_attn_in = _L0_attn_setup()

    def _L0_ffn_setup():
        import jax, jax.numpy as jnp
        import numpy as np
        E = 64
        K = 6
        CAP = 128
        SCALE = 1.0
        H = 512
        I = 192
        SI = I * 2
        B, S = (2, 256)

        def _moe(x, gate_w, gate_up_proj, down_proj, shared_gate_w, shared_up_w, shared_down_w):
            b, s, h = x.shape
            T = b * s
            xf = x.reshape(T, h)
            scores = jax.nn.softmax(xf @ gate_w.T, axis=-1)
            topk_w, topk_idx = jax.lax.top_k(scores, K)
            topk_w = topk_w * SCALE
            flat_e = topk_idx.reshape(-1)
            order = jnp.argsort(flat_e)
            sorted_e = flat_e[order]
            sorted_tok = (order // K).astype(jnp.int32)
            sorted_w = topk_w.reshape(-1)[order]
            counts = jnp.zeros((E,), jnp.int32).at[flat_e].add(1)
            offsets = jnp.cumsum(counts) - counts
            pos = jnp.arange(T * K, dtype=jnp.int32) - offsets[sorted_e]
            buf_tok = jnp.full((E, CAP), T, jnp.int32).at[sorted_e, pos].set(sorted_tok, mode='drop')
            buf_w = jnp.zeros((E, CAP), x.dtype).at[sorted_e, pos].set(sorted_w, mode='drop')
            xp = jnp.concatenate([xf, jnp.zeros((1, h), x.dtype)], axis=0)
            gx = xp[buf_tok]
            gu = jnp.einsum('ech,ehi->eci', gx, gate_up_proj)
            g, u = jnp.split(gu, 2, axis=-1)
            hid = jax.nn.silu(g) * u
            eo = jnp.einsum('eci,eih->ech', hid, down_proj) * buf_w[..., None]
            routed = jnp.zeros((T + 1, h), x.dtype).at[buf_tok.reshape(-1)].add(eo.reshape(-1, h))[:T]
            shared = jax.nn.silu(xf @ shared_gate_w.T) * (xf @ shared_up_w.T) @ shared_down_w.T
            return (routed + shared).reshape(b, s, h)
        key = jax.random.key(seed)
        ks = jax.random.split(key, 7)
        x = jax.random.normal(ks[0], (B, S, H), jnp.float32)
        gate_w = jax.random.normal(ks[1], (E, H), jnp.float32) * 0.02
        gate_up_proj = jax.random.normal(ks[2], (E, H, 2 * I), jnp.float32) * 0.02
        down_proj = jax.random.normal(ks[3], (E, I, H), jnp.float32) * 0.02
        shared_gate_w = jax.random.normal(ks[4], (SI, H), jnp.float32) * 0.02
        shared_up_w = jax.random.normal(ks[5], (SI, H), jnp.float32) * 0.02
        shared_down_w = jax.random.normal(ks[6], (H, SI), jnp.float32) * 0.02
        return dict(x=x, gate_w=gate_w, gate_up_proj=gate_up_proj, down_proj=down_proj, shared_gate_w=shared_gate_w, shared_up_w=shared_up_w, shared_down_w=shared_down_w)
    _L0_ffn_in = _L0_ffn_setup()
    _d = {'L0_attn_x': _L0_attn_in['x'], 'L0_attn_w_qkv': _L0_attn_in['w_qkv'], 'L0_attn_w_out': _L0_attn_in['w_out'], 'L0_attn_decay_param': _L0_attn_in['decay_param'], 'L0_ffn_gate_w': _L0_ffn_in['gate_w'], 'L0_ffn_gate_up_proj': _L0_ffn_in['gate_up_proj'], 'L0_ffn_down_proj': _L0_ffn_in['down_proj'], 'L0_ffn_shared_gate_w': _L0_ffn_in['shared_gate_w'], 'L0_ffn_shared_up_w': _L0_ffn_in['shared_up_w'], 'L0_ffn_shared_down_w': _L0_ffn_in['shared_down_w']}
    _x0 = _d['L0_attn_x']
    _d['L0_attn_x'] = jax.random.normal(jax.random.fold_in(jax.random.key(seed), 1), (1, 4096, 512), dtype=_x0.dtype)
    del _x0
    return _d

def reference(L0_attn_x, L0_attn_w_qkv, L0_attn_w_out, L0_attn_decay_param, L0_ffn_gate_w, L0_ffn_gate_up_proj, L0_ffn_down_proj, L0_ffn_shared_gate_w, L0_ffn_shared_up_w, L0_ffn_shared_down_w):

    def _L0_attn_ref(x, w_qkv, w_out, decay_param):
        import jax, jax.numpy as jnp
        import numpy as np
        H = 16
        EPS_DEN = 1e-06

        def _decay_scan(x, decay, init):
            xT = jnp.moveaxis(x, 2, 0)

            def step(s, xt):
                s = decay * s + xt
                return (s, s)
            _, ys = jax.lax.scan(step, init, xT)
            return jnp.moveaxis(ys, 0, 2)

        def _phi(z):
            return jax.nn.elu(z) + 1.0

        def _reference_tuple_inner(x, w_qkv, w_out, decay_param):
            B, T, Hid = x.shape
            D = Hid // H
            qkv = x @ w_qkv
            q, k, v = jnp.split(qkv, 3, axis=-1)

            def to_bhtd(t):
                return t.reshape(B, T, H, D).transpose(0, 2, 1, 3)
            q = _phi(to_bhtd(q))
            k = _phi(to_bhtd(k))
            v = to_bhtd(v)
            decay = jax.nn.sigmoid(decay_param).reshape(1, H, 1)
            init = jnp.zeros((B, H, D), dtype=x.dtype)
            running_kv = _decay_scan(k * v, decay, init)
            running_ksum = _decay_scan(k, decay, init)
            den = jnp.clip(jnp.sum(q * running_ksum, axis=-1, keepdims=True), EPS_DEN, None)
            out = q * running_kv / den
            out = out.transpose(0, 2, 1, 3).reshape(B, T, Hid) @ w_out
            new_kv = running_kv[:, :, -1, :]
            new_ksum = running_ksum[:, :, -1, :]
            return (out, new_kv, new_ksum)
        return _reference_tuple_inner(x, w_qkv, w_out, decay_param)[0]

    def _L0_ffn_ref(x, gate_w, gate_up_proj, down_proj, shared_gate_w, shared_up_w, shared_down_w):
        import jax, jax.numpy as jnp
        import numpy as np
        E = 64
        K = 6
        CAP = 128
        SCALE = 1.0
        H = 512
        I = 192
        SI = I * 2
        B, S = (2, 256)

        def _moe(x, gate_w, gate_up_proj, down_proj, shared_gate_w, shared_up_w, shared_down_w):
            b, s, h = x.shape
            T = b * s
            xf = x.reshape(T, h)
            scores = jax.nn.softmax(xf @ gate_w.T, axis=-1)
            topk_w, topk_idx = jax.lax.top_k(scores, K)
            topk_w = topk_w * SCALE
            flat_e = topk_idx.reshape(-1)
            order = jnp.argsort(flat_e)
            sorted_e = flat_e[order]
            sorted_tok = (order // K).astype(jnp.int32)
            sorted_w = topk_w.reshape(-1)[order]
            counts = jnp.zeros((E,), jnp.int32).at[flat_e].add(1)
            offsets = jnp.cumsum(counts) - counts
            pos = jnp.arange(T * K, dtype=jnp.int32) - offsets[sorted_e]
            buf_tok = jnp.full((E, CAP), T, jnp.int32).at[sorted_e, pos].set(sorted_tok, mode='drop')
            buf_w = jnp.zeros((E, CAP), x.dtype).at[sorted_e, pos].set(sorted_w, mode='drop')
            xp = jnp.concatenate([xf, jnp.zeros((1, h), x.dtype)], axis=0)
            gx = xp[buf_tok]
            gu = jnp.einsum('ech,ehi->eci', gx, gate_up_proj)
            g, u = jnp.split(gu, 2, axis=-1)
            hid = jax.nn.silu(g) * u
            eo = jnp.einsum('eci,eih->ech', hid, down_proj) * buf_w[..., None]
            routed = jnp.zeros((T + 1, h), x.dtype).at[buf_tok.reshape(-1)].add(eo.reshape(-1, h))[:T]
            shared = jax.nn.silu(xf @ shared_gate_w.T) * (xf @ shared_up_w.T) @ shared_down_w.T
            return (routed + shared).reshape(b, s, h)
        return _moe(x, gate_w, gate_up_proj, down_proj, shared_gate_w, shared_up_w, shared_down_w)
    x = L0_attn_x
    x = _layernorm(x + _L0_attn_ref(x, L0_attn_w_qkv, L0_attn_w_out, L0_attn_decay_param), axis=-1)
    x = _layernorm(x + _L0_ffn_ref(x, L0_ffn_gate_w, L0_ffn_gate_up_proj, L0_ffn_down_proj, L0_ffn_shared_gate_w, L0_ffn_shared_up_w, L0_ffn_shared_down_w), axis=-1)
    return x

_drawn_inputs = setup_inputs


def setup_inputs(seed=0):
    import zlib

    import numpy as np

    out = dict(_drawn_inputs(seed))
    spreads = {'L0_attn_decay_param': (0.949999988079071, 0.6)}
    factors = {'L0_attn_w_qkv': 8.0,
     'L0_attn_w_out': 8.0,
     'L0_ffn_gate_w': 8.0,
     'L0_ffn_gate_up_proj': 8.0,
     'L0_ffn_down_proj': 8.0}
    for name, (base, spread) in spreads.items():
        noise = np.random.default_rng([zlib.crc32(name.encode()), seed]).standard_normal(out[name].shape)
        drawn = base * np.exp(spread * noise) if base else spread * noise
        out[name] = jnp.asarray(drawn.astype(out[name].dtype))
    for name, factor in factors.items():
        out[name] = (out[name] * factor).astype(out[name].dtype)
    return out
```

```python
from contextlib import ExitStack

import numpy as np

import concourse.bass as bass
from concourse import mybir

F32 = mybir.dt.float32
F32R = mybir.dt.float32r
BF16 = mybir.dt.bfloat16
U32 = mybir.dt.uint32
ALU = mybir.AluOpType
ACT = mybir.ActivationFunctionType
AX = mybir.AxisListType

P = 128
HEADS = 16
TOP_K = 6
CAP = 128
EPS_NORM = 1e-5
EPS_DEN = 1e-6


class Queue:

    def __init__(self, name, sem):
        self.name, self.sem, self.count, self.items, self.seen = name, sem, 0, [], {}

    def wait(self, *ticks):
        for tick in ticks:
            if tick is None:
                continue
            sem, value = tick
            if self.seen.get(id(sem), 0) < value:
                self.seen[id(sem)] = value
                self.items.append((None, sem, value))

    def do(self, make, *ticks):
        self.wait(*ticks)
        self.count += 1
        self.items.append((make, self.sem, 1))
        return self.sem, self.count

    def quiet(self, make, *ticks):
        self.wait(*ticks)
        self.items.append((make, None, 0))

    def dma(self, make, lane, *ticks):
        self.wait(*ticks)
        lane.count += 16
        self.items.append((make, lane.sem, 16))
        return lane.sem, lane.count

    def flush(self, engine):
        for make, sem, value in self.items:
            if make is None:
                engine.wait_ge(sem, value)
            elif sem is None:
                make()
            else:
                make().then_inc(sem, value)


class Lane:

    def __init__(self, sem):
        self.sem, self.count = sem, 0


class Ring:

    def __init__(self, buffers):
        self.buffers, self.left, self.n = buffers, [() for _ in buffers], 0

    def take(self):
        slot = self.n % len(self.buffers)
        self.n += 1
        left, self.left[slot] = self.left[slot], None
        assert left is not None, "the slot's last use has not been left"
        return slot, self.buffers[slot], left

    def leave(self, slot, *ticks):
        self.left[slot] = ticks


class Map:

    def __init__(self, nc, start, end):
        self.nc, self.at, self.end = nc, start, end

    def place(self, name, shape, dt=F32):
        size = int(np.prod(shape[1:])) * (2 if dt == BF16 else 4)
        offset = self.at
        self.at += (size + 31) // 32 * 32
        assert self.at <= self.end, (name, self.at, self.end)
        return self.nc.alloc_sbuf_tensor_at(name, shape, dt, offset=offset)


def build(nc, x, x_t, w_qkv, w_out, decay_param, gate_t, w_gu, w_down, sg_t, su_t, sd_t, out):
    T, D = x.shape
    E, _, GU = w_gu.shape
    I = GU // 2
    SI = sg_t.shape[1]
    BT = 512
    NB = T // BT
    NJ = BT // P
    NT = T // P
    KC = D // P
    SC = SI // P
    IH = I // 2
    SLOTS = E * CAP
    HW = D // HEADS
    TAIL = 2
    NW = 5
    assert SC < NJ and KC == NJ and SI == GU

    x1_dram = nc.dram_tensor("x1_rows", (T, D), F32, kind="Internal").ap()
    x1t_dram = nc.dram_tensor("x1_turned", (D, T), F32, kind="Internal").ap()
    acc_dram = nc.dram_tensor("acc_rows", (T, D), F32, kind="Internal").ap()
    table_dram = nc.dram_tensor("slot_table", (SLOTS, 2), U32, kind="Internal").ap()

    start, end = (nc.sbuf_base + 31) // 32 * 32, nc.sbuf_usable_end
    both = Map(nc, start, end)
    ident = both.place("ident", [P, P])
    minus_half = both.place("minus_half", [P, 1])
    table_sb = both.place("table_sb", [P, E, 2], U32)
    stats = both.place("stats", [P, 6])
    mv = [both.place(f"mv{i}", [P, 2]) for i in range(2)]
    rstd = [both.place(f"rstd{i}", [P, 1]) for i in range(2)]
    wgu_buf = [both.place(f"wgu{i}", [P, KC, GU]) for i in range(2)]
    wdn_buf = [both.place(f"wdn{i}", [IH, 2, D]) for i in range(2)]

    att = Map(nc, both.at, end)
    wqkv_hi = att.place("wqkv_hi", [P, 3 * KC, KC, P], F32R)
    wqkv_lo = att.place("wqkv_lo", [P, 3 * KC, KC, P], F32R)
    x_stage = [att.place(f"x_stage{i}", [P, BT]) for i in range(2)]
    x_hi = [att.place(f"x_hi{i}", [P, KC, BT], F32R) for i in range(2)]
    x_lo = [att.place(f"x_lo{i}", [P, KC, BT], F32R) for i in range(2)]
    projected_end = att.at
    wout_hi = att.place("wout_hi", [P, KC, D], F32R)
    wout_lo = att.place("wout_lo", [P, KC, D], F32R)
    gate_sb = att.place("gate_sb", [P, KC, E])
    before = att.place("before", [P, P], BF16)
    not_before = att.place("not_before", [P, P], BF16)
    ones = att.place("ones", [P, P], BF16)
    head_sum = att.place("head_sum", [P, KC, HEADS])
    head_send = att.place("head_send", [HEADS, KC, P], F32R)
    expert_no = att.place("expert_no", [P, E], BF16)
    decay = att.place("decay", [P, KC])
    xres = [att.place(f"xres{i}", [P, D]) for i in range(2)]
    e_sb = [att.place(f"e{i}", [P, BT]) for i in range(2)]
    relu_sb = [att.place("relu", [P, BT])]
    phi_k = att.place("phi_k", [P, BT])
    kv = att.place("kv", [P, BT])
    run_k = att.place("run_k", [P, BT])
    run_kv = att.place("run_kv", [P, BT])
    phi_q = att.place("phi_q", [P, BT])
    qk = [att.place(f"qk{i}", [P, BT]) for i in range(KC + 1)]
    state = att.place("state", [P, KC, 2])
    num = [att.place(f"num{i}", [P, BT]) for i in range(KC + 2)]
    att_hi = att.place("att_hi", [P, KC, BT], F32R)
    att_lo = att.place("att_lo", [P, KC, BT], F32R)
    rden = att.place("rden", [P, NJ, HEADS])
    rden_hi = att.place("rden_hi", [HEADS, BT], F32R)
    rden_lo = att.place("rden_lo", [HEADS, BT], F32R)
    x1_sb = [att.place(f"x1_{i}", [P, D]) for i in range(NJ)]
    x1t_sb = [att.place(f"x1t{i}", [P, KC, P]) for i in range(2)]
    neg_max = att.place("neg_max", [P, 1])
    e_route = att.place("e_route", [P, E])
    e_sum = att.place("e_sum", [P, 1])
    r_sum = att.place("r_sum", [P, 1])
    score = att.place("score", [P, E])
    top_v = att.place("top_v", [P, 8])
    top_i = att.place("top_i", [P, 8], U32)
    top_if = att.place("top_if", [P, TOP_K])
    chosen = [att.place(f"chosen{i}", [P, TOP_K, E], BF16) for i in range(2)]
    placed = att.place("placed", [P, TOP_K, E])
    place = att.place("place", [P, TOP_K])
    slot_of = att.place("slot_of", [P, NT, TOP_K], U32)
    pairs = att.place("pairs", [P, NT, TOP_K, 2], U32)

    exp = Map(nc, both.at, projected_end)
    sg_hi = exp.place("sg_hi", [P, KC, SI], F32R)
    sg_lo = exp.place("sg_lo", [P, KC, SI], F32R)
    su_hi = exp.place("su_hi", [P, KC, SI], F32R)
    su_lo = exp.place("su_lo", [P, KC, SI], F32R)
    sd_hi = exp.place("sd_hi", [P, SC, D], F32R)
    sd_lo = exp.place("sd_lo", [P, SC, D], F32R)
    x1t_stage = exp.place("x1t_stage", [P, KC, BT])
    x1t_hi = exp.place("x1t_hi", [P, KC, BT], F32R)
    x1t_lo = exp.place("x1t_lo", [P, KC, BT], F32R)
    hid_hi = exp.place("hid_hi", [P, SC, BT], F32R)
    hid_lo = exp.place("hid_lo", [P, SC, BT], F32R)
    tanh_s = exp.place("tanh_s", [P, BT])
    silu_s = exp.place("silu_s", [P, BT])
    hid_s = exp.place("hid_s", [P, BT])
    late = Map(nc, projected_end, end)
    shared_rows = [late.place(f"shared_rows{b}", [P, NJ, D]) for b in range(NB - TAIL)]
    wgu_buf += [late.place(f"wgu{i}", [P, KC, GU]) for i in range(2, NW)]
    wdn_buf += [late.place(f"wdn{i}", [IH, 2, D]) for i in range(2, NW)]
    xg = [late.place(f"xg{i}", [P, D]) for i in range(3)]
    xgt = [late.place(f"xgt{i}", [P, KC, P]) for i in range(2)]
    eo = [late.place(f"eo{i}", [P, D]) for i in range(3)]
    tanh_e = late.place("tanh_e", [P, I])
    silu_e = late.place("silu_e", [P, I])
    hid_e = [late.place(f"hid_e{i}", [P, I]) for i in range(2)]
    hid_et = [late.place(f"hid_et{i}", [IH, 2, P]) for i in range(2)]
    fin_map = Map(nc, both.at - 2 * 4 * (KC * GU + 2 * D), both.at)
    fin_sb = [fin_map.place(f"fin{i}", [P, NJ, D]) for i in range(2)]

    ctx = ExitStack()
    with ctx:
        def sem(name):
            return ctx.enter_context(nc.semaphore(name))

        banks = [ctx.enter_context(nc.psum_tensor(f"bank{i}", [P, 512], F32)) for i in range(8)]

        PE = Queue("PE", sem("pe"))
        DVE = Queue("DVE", sem("dve"))
        SCA = Queue("ACT", sem("act"))
        POOL = Queue("POOL", sem("pool"))
        SP = Queue("SP", None)
        V, S, G, M, Y = nc.vector, nc.scalar, nc.gpsimd, nc.tensor, nc.sync
        last = {}

        def lanes(name, n):
            return [Lane(sem(f"{name}{i}")) for i in range(n)]

        def load(name, dst, src, *ticks):
            return SP.dma(lambda: Y.dma_start(dst, src), Lane(sem(f"ld_{name}")), *ticks)

        def split(hi, lo, src, t_src, *left):
            t_hi = SCA.do(lambda: S.copy(hi, src), t_src, *left)
            t_lo = DVE.do(lambda: V.tensor_tensor(lo, src, hi.bitcast(F32), ALU.subtract), t_hi, t_src, *left)
            return t_hi, t_lo

        def group(out_ap, products, *ticks):
            n = len(products)
            for i, (a, b) in enumerate(products):
                make = lambda a=a, b=b, i=i: M.matmul(out_ap, a, b, start=(i == 0), stop=(i == n - 1))
                PE.wait(*(ticks if i == 0 else ()))
                t = PE.do(make) if i == n - 1 else PE.quiet(make)
            return t

        def three(a_hi, a_lo, b_hi, b_lo):
            return [(a_hi, b_hi), (a_hi, b_lo), (a_lo, b_hi)]

        t = POOL.do(lambda: G.memset(ident[:, :], 0.0))
        t_ident = POOL.do(lambda: G.affine_select(
            out=ident[:, :], in_=ident[:, :], compare_op=ALU.not_equal, fill=1.0, base=0,
            pattern=[[-1, P]], channel_multiplier=1), t)
        t_ones = POOL.do(lambda: G.memset(ones[:, :], 1.0))
        t_before = POOL.do(lambda: G.affine_select(
            out=before[:, :], in_=ones[:, :], compare_op=ALU.is_ge, fill=0.0, base=-1,
            pattern=[[1, P]], channel_multiplier=-1), t_ones)
        t_before = POOL.do(lambda: G.affine_select(
            out=not_before[:, :], in_=ones[:, :], compare_op=ALU.is_ge, fill=0.0, base=0,
            pattern=[[-1, P]], channel_multiplier=1), t_ones)

        per_chunk = P // HW

        def head_mask(buf, rows_are_channels):
            t = POOL.do(lambda: G.memset(buf, 1.0))
            for sign, base in ((1, 0), (-1, HW - 1)):
                if rows_are_channels:
                    pattern, mult = [[sign * HW * per_chunk, KC], [-sign * HW, HEADS]], sign
                else:
                    pattern, mult = [[sign * HW * per_chunk, KC], [sign, P]], -sign * HW
                t = POOL.do(lambda pattern=pattern, mult=mult, base=base: G.affine_select(
                    out=buf, in_=buf, compare_op=ALU.is_ge, fill=0.0, base=base,
                    pattern=pattern, channel_multiplier=mult), t)
            return t

        t_sum = head_mask(head_sum[:, :, :], True)
        mask_f = kv[0:HEADS, :].rearrange("p (k c) -> p k c", k=KC)
        t = head_mask(mask_f, False)
        t_send = POOL.do(lambda: G.tensor_copy(head_send[:, :, :], mask_f), t)
        last["kv"] = (t_send,)
        t_expert_no = POOL.do(lambda: G.iota(expert_no[:, :], pattern=[[1, E]], base=0, channel_multiplier=0,
                                             allow_small_or_imprecise_dtypes=True))
        t_half = POOL.do(lambda: G.memset(minus_half[:, :], -0.5))
        t_token = POOL.do(lambda: G.iota(pairs[:, :, :, 0], pattern=[[P, NT], [0, TOP_K]], base=0,
                                         channel_multiplier=1))
        t1 = POOL.do(lambda: G.iota(table_sb[:, :, 0], pattern=[[0, E]], base=T, channel_multiplier=0))
        t2 = POOL.do(lambda: G.iota(table_sb[:, :, 1], pattern=[[0, E]], base=0, channel_multiplier=0))
        table_v = table_dram.rearrange("(s e) w -> s e w", e=E)

        num_ring = Ring(num)
        stage_lane = lanes("stage_lane", len(num))
        wq_v = w_qkv.rearrange("(k p) n -> p k n", p=P)
        wqkv_ready, wout_ready = {}, {}

        def stage_weights(key, src, hi, lo, ready):
            slot, buf, left = num_ring.take()
            shape = buf[:, :]
            view = shape if len(hi.shape) == 2 else shape.rearrange("p (k n) -> p k n", k=KC)
            t = SP.dma(lambda: Y.dma_start(view, src), stage_lane[slot], *left)
            ticks = split(hi, lo, view, t)
            num_ring.leave(slot, *ticks)
            ready[key] = ticks

        x_ring, x_lane = Ring(x_stage), lanes("x_lane", 2)
        x_staged, x_ready, x_left = {}, {}, {}

        def load_x(b, k):
            slot, buf, left = x_ring.take()
            src = x_t[k * P:(k + 1) * P, b * BT:(b + 1) * BT]
            x_staged[b, k] = slot, buf, SP.dma(lambda: Y.dma_start(buf[:, :], src), x_lane[slot], *left)

        def split_x(b, k):
            i = b % 2
            slot, buf, t = x_staged[b, k]
            x_ready[b, k] = split(x_hi[i][:, k, :], x_lo[i][:, k, :], buf[:, :], t, x_left.get(b - 2))
            x_ring.leave(slot, *x_ready[b, k])

        decay_in = load("decay", decay[:, :], decay_param)
        load_x(0, 0)
        load_x(0, 1)
        PARTS = (1, 2, 0)
        for c in range(KC):
            for n, part in enumerate(PARTS):
                cols = slice(part * D + c * P, part * D + (c + 1) * P)
                i = 3 * c + n
                stage_weights((c, n), wq_v[:, :, cols], wqkv_hi[:, i, :, :], wqkv_lo[:, i, :, :], wqkv_ready)
                if i == 0:
                    for k in range(KC):
                        split_x(0, k)
                        if k + 2 < KC:
                            load_x(0, k + 2)
        load_x(1, 0)
        load_x(1, 1)
        for c in range(KC):
            stage_weights(c, w_out[c * P:(c + 1) * P, :], wout_hi[:, c, :], wout_lo[:, c, :], wout_ready)
        gate_in = load("gate", gate_sb[:, :, :], gate_t.rearrange("(k p) n -> p k n", p=P))
        table_empty = load("table_empty", table_v, table_sb[:, :, :], t1, t2)
        t = SCA.do(lambda: S.activation(decay[:, :], decay[:, :], ACT.Exp, scale=-1.0), decay_in)
        t = DVE.do(lambda: V.tensor_scalar(decay[:, :], decay[:, :], 1.0, None, ALU.add), t)
        t_decay = DVE.do(lambda: V.reciprocal(decay[:, :], decay[:, :]), t)
        t_state = DVE.do(lambda: V.memset(state[:, :, :], 0.0))

        ps_proj = Ring(banks[0:3])
        e_ring, relu_ring, qk_ring = Ring(e_sb), Ring(relu_sb), Ring(qk)
        num_ready, qk_ready, state_tick = {}, {}, {}

        def project_group(b, c, n):
            slot, ps, left = ps_proj.take()
            xh, xl = x_hi[b % 2], x_lo[b % 2]
            i = 3 * c + n
            products = []
            for k in range(KC):
                products += three(wqkv_hi[:, i, k, :], wqkv_lo[:, i, k, :], xh[:, k, :], xl[:, k, :])
            ready = [t for k in range(KC) for t in x_ready[b, k]] if (c, n) == (0, 0) else []
            mm = group(ps[:, :], products, *ready, *wqkv_ready[c, n], *left)
            return slot, ps, mm

        def feature_map(dst, n, b, c, *dst_left):
            slot, ps, mm = project_group(b, c, n)
            es, e, e_left = e_ring.take()
            rs, r, r_left = relu_ring.take()
            te = SCA.do(lambda: S.activation(e[:, :], ps[:, :], ACT.Exp), mm, *e_left)
            tr = SCA.do(lambda: S.activation(r[:, :], ps[:, :], ACT.Relu), *r_left)
            ps_proj.leave(slot, tr)
            t = DVE.do(lambda: V.scalar_tensor_tensor(out=dst[:, :], in0=e[:, :], scalar=1.0, in1=r[:, :],
                                                      op0=ALU.min, op1=ALU.add), te, tr, *dst_left)
            e_ring.leave(es, t)
            relu_ring.leave(rs, t)
            return t, mm

        running = {}

        def project_k(b, c):
            running["k"], _ = feature_map(phi_k, 0, b, c, *last.get("phi_k", ()))

        def scan_k(b, c):
            dec = decay[:, c:c + 1].to_broadcast([P, BT])
            running["rk"] = DVE.do(lambda: V.tensor_tensor_scan(
                out=run_k[:, :], data0=dec, data1=phi_k[:, :], initial=state[:, c, 0:1],
                op0=ALU.mult, op1=ALU.add), running["k"], t_decay, t_state, state_tick.get(c), *last.get("run_k", ()))

        def project_v(b, c):
            running["v"] = project_group(b, c, 1)

        def scan_kv(b, c):
            slot, ps, mm_v = running["v"]
            dec = decay[:, c:c + 1].to_broadcast([P, BT])
            t_kv = DVE.do(lambda: V.tensor_tensor(kv[:, :], phi_k[:, :], ps[:, :], ALU.mult),
                          mm_v, *last.get("kv", ()))
            ps_proj.leave(slot, t_kv)
            last["phi_k"] = (running["rk"], t_kv)
            running["rkv"] = DVE.do(lambda: V.tensor_tensor_scan(
                out=run_kv[:, :], data0=dec, data1=kv[:, :], initial=state[:, c, 1:2],
                op0=ALU.mult, op1=ALU.add), t_kv, *last.get("run_kv", ()))
            last["kv"] = (running["rkv"],)

        def project_q(b, c):
            t_q, mm_q = feature_map(phi_q, 2, b, c, *last.get("phi_q", ()))
            if c == KC - 1:
                x_left[b] = mm_q
            t_sk = SCA.do(lambda: S.copy(state[:, c, 0:1], run_k[:, BT - 1:BT]), running["rk"])
            t_skv = SCA.do(lambda: S.copy(state[:, c, 1:2], run_kv[:, BT - 1:BT]), running["rkv"])
            state_tick[c] = t_skv
            qs, qkb, q_left = qk_ring.take()
            t_qk = DVE.do(lambda: V.tensor_tensor(qkb[:, :], phi_q[:, :], run_k[:, :], ALU.mult), t_q, *q_left)
            ns, nm, n_left = num_ring.take()
            t_num = POOL.do(lambda: G.tensor_tensor(nm[:, :], phi_q[:, :], run_kv[:, :], ALU.mult),
                            t_q, running["rkv"], *n_left)
            last["run_k"] = (t_qk, t_sk)
            last["run_kv"] = (t_num, t_skv)
            last["phi_q"] = (t_qk, t_num)
            qk_ready[b, c] = (qs, qkb, t_qk)
            num_ready[b, c] = (ns, nm, t_num)

        ps_send, ps_small = Ring(banks[6:7]), Ring(banks[5:6])
        den_tick, att_ready, att_left = {}, {}, {}

        def sum_heads(b):
            slot, ps, left = ps_small.take()
            for j in range(NJ):
                mm = group(ps[:, j * HEADS:(j + 1) * HEADS],
                           [(qk_ready[b, c][1][:, j * P:(j + 1) * P], head_sum[:, c, :]) for c in range(KC)],
                           *[qk_ready[b, c][2] for c in range(KC)], t_sum, *left)
            for c in range(KC):
                qk_ring.leave(qk_ready[b, c][0], mm)
            flat = rden[:, :, :].rearrange("p j h -> p (j h)")
            t = DVE.do(lambda: V.tensor_scalar(flat, ps[:, 0:NJ * HEADS], EPS_DEN, None, ALU.max),
                       mm, *last.get("rden", ()))
            ps_small.leave(slot, t)
            den_tick[b] = DVE.do(lambda: V.reciprocal(flat, flat), t)

        def turn_rden(b):
            slot, ps, left = ps_small.take()
            PE.wait(den_tick[b], t_ident, *left)
            for j in range(NJ):
                make = lambda j=j: M.transpose(ps[0:HEADS, j * P:(j + 1) * P], rden[:, j, :], ident[:, :])
                mm = PE.do(make) if j == NJ - 1 else PE.quiet(make)
            last["rden"] = (mm,)
            den_tick[b] = split(rden_hi[:, :], rden_lo[:, :], ps[0:HEADS, :], mm, *last.get("rden_hi", ()))
            ps_small.leave(slot, *den_tick[b])

        def divide(b, c):
            slot, ps, left = ps_send.take()
            mm = group(ps[:, :], [(head_send[:, c, :], rden_hi[:, :]), (head_send[:, c, :], rden_lo[:, :])],
                       t_send, *den_tick[b], *left)
            ns, nm, t_num = num_ready[b, c]
            t = DVE.do(lambda: V.tensor_tensor(nm[:, :], nm[:, :], ps[:, :], ALU.mult), mm, t_num)
            ps_send.leave(slot, t)
            last["rden_hi"] = (mm,)
            att_ready[b, c] = split(att_hi[:, c, :], att_lo[:, c, :], nm[:, :], t, att_left.get(b - 1))
            num_ring.leave(ns, *att_ready[b, c])

        xres_ring, xres_lane, xres_ready = Ring(xres), lanes("xres_lane", len(xres)), {}

        def load_xres(b, j):
            slot, buf, left = xres_ring.take()
            row = b * BT + j * P
            t = SP.dma(lambda: Y.dma_start(buf[:, :], x[row:row + P, :]), xres_lane[slot], *left)
            xres_ready[b, j] = (slot, buf, t)

        norms = [0]

        def norm(buf, t_src):
            i = norms[0] % 2
            norms[0] += 1
            t = DVE.do(lambda: V.bn_stats(stats[:, :], buf), t_src, *last.get("stats", ()))
            t_mv = DVE.do(lambda: V.bn_aggr(mv[i][:, :], stats[:, :]), t, *last.get(f"mv{i}", ()))
            last["stats"] = (t_mv,)
            t = POOL.do(lambda: G.tensor_scalar(rstd[i][:, :], mv[i][:, 1:2], EPS_NORM, None, ALU.add),
                        t_mv, *last.get(f"mv{i}", ()))
            t_r = POOL.do(lambda: G.tensor_tensor(rstd[i][:, :], rstd[i][:, :], minus_half[:, :], ALU.pow), t, t_half)

            def apply():
                t = DVE.do(lambda: V.tensor_scalar(buf, buf, mv[i][:, 0:1], rstd[i][:, 0:1],
                                                   ALU.subtract, ALU.mult), t_r, t_mv)
                last[f"mv{i}"] = (t,)
                return t
            return apply

        ps_rows_a = Ring(banks[4:5])
        x1_ring, x1_lane = Ring(x1_sb), lanes("x1_lane", len(x1_sb))
        acc_lane = lanes("acc_lane", len(x1_sb))
        x1_ready, x1_stored, x1_open = {}, [], []

        def out_project(b, j):
            slot, ps, left = ps_rows_a.take()
            tok = slice(j * P, (j + 1) * P)
            products = []
            for k in range(KC):
                products += three(att_hi[:, k, tok], att_lo[:, k, tok], wout_hi[:, k, :], wout_lo[:, k, :])
            ready = [t for c in range(KC) for t in (*att_ready[b, c], *wout_ready[c])]
            mm = group(ps[:, :], products, *ready, *left)
            if j == NJ - 1:
                att_left[b] = mm
            xs, xr, t_x = xres_ready[b, j]
            x1s, x1, x1_left = x1_ring.take()
            t = DVE.do(lambda: V.tensor_tensor(x1[:, :], ps[:, :], xr[:, :], ALU.add), mm, t_x, *x1_left)
            ps_rows_a.leave(slot, t)
            xres_ring.leave(xs, t)
            x1_open.append((b, j, x1s, x1, norm(x1[:, :], t)))

        def store_x1():
            b, j, x1s, x1, apply = x1_open.pop(0)
            t = apply()
            row = b * BT + j * P
            w1 = SP.dma(lambda: Y.dma_start(x1_dram[row:row + P, :], x1[:, :]), x1_lane[x1s], t)
            w2 = SP.dma(lambda: Y.dma_start(acc_dram[row:row + P, :], x1[:, :]), acc_lane[x1s], t)
            x1_stored.extend((w1, w2))
            x1_ready[b, j] = (x1s, x1, t, w1, w2)

        ps_turn, ps_count = Ring(banks[3:4]), banks[7]
        x1t_ring, x1t_lane, x1t_stored = Ring(x1t_sb), lanes("x1t_lane", len(x1t_sb)), {}
        chosen_ring = Ring(chosen)
        scatter_lane = Lane(sem("scatter_lane"))
        scattered = []

        turned, routing = {}, {}

        def turn(b, j):
            slot, ps, left = ps_turn.take()
            x1s, x1, t_x1, w1, w2 = x1_ready[b, j]
            PE.wait(t_x1, t_ident, *left)
            for k in range(KC):
                make = lambda k=k: M.transpose(ps[:, k * P:(k + 1) * P], x1[:, k * P:(k + 1) * P], ident[:, :])
                mm = PE.do(make) if k == KC - 1 else PE.quiet(make)
            x1_ring.leave(x1s, mm, w1, w2)
            ts, x1t, t_left = x1t_ring.take()
            t = SCA.do(lambda: S.copy(x1t[:, :, :], ps[:, :].rearrange("p (k t) -> p k t", k=KC)), mm, *t_left)
            ps_turn.leave(slot, t)
            col = b * BT + j * P
            dst = x1t_dram.rearrange("(k p) t -> p k t", p=P)[:, :, col:col + P]
            w = SP.dma(lambda: Y.dma_start(dst, x1t[:, :, :]), x1t_lane[ts], t)
            x1t_stored[b, j] = w
            turned[b, j] = (ts, x1t, t, w)

        def score_experts(b, j):
            ts, x1t, t, w = turned[b, j]
            slot, logits, left = ps_small.take()
            mm = group(logits[:, 0:E], [(x1t[:, k, :], gate_sb[:, k, :]) for k in range(KC)], t, gate_in, *left)
            x1t_ring.leave(ts, mm, w)
            t = DVE.do(lambda: V.tensor_reduce(neg_max[:, :], logits[:, 0:E], AX.X, ALU.max, negate=True),
                       mm, *last.get("neg_max", ()))
            t_e = SCA.do(lambda: S.activation(e_route[:, :], logits[:, 0:E], ACT.Exp, bias=neg_max[:, 0:1],
                                              accum_out=e_sum[:, :]), t, *last.get("e_route", ()))
            last["neg_max"] = (t_e,)
            ps_small.leave(slot, t_e)
            routing[b, j] = t_e

        def choose(b, j):
            i = b * NJ + j
            t_e = routing[b, j]
            t = DVE.do(lambda: V.reciprocal(r_sum[:, :], e_sum[:, :]), t_e, *last.get("r_sum", ()))
            t_s = DVE.do(lambda: V.tensor_scalar(score[:, :], e_route[:, :], r_sum[:, 0:1], None, ALU.mult),
                         t, *last.get("score", ()))
            last["e_route"] = last["r_sum"] = (t_s,)
            t_v = DVE.do(lambda: V.max(top_v[:, :], score[:, :]), t_s, *last.get("top_v", ()))
            t_i = DVE.do(lambda: V.max_index(top_i[:, :], top_v[:, :], score[:, :]), t_v, *last.get("top_i", ()))
            last["score"] = (t_i,)
            t_w = SCA.do(lambda: S.copy(pairs[:, i, :, 1].bitcast(F32), top_v[:, 0:TOP_K]), t_v, t_token)
            last["top_v"] = (t_w, t_i)
            t_f = DVE.do(lambda: V.tensor_copy(top_if[:, :], top_i[:, 0:TOP_K]), t_i, *last.get("top_if", ()))
            last["top_i"] = (t_f,)
            cs, ch, c_left = chosen_ring.take()
            t_c = DVE.do(lambda: V.tensor_tensor(
                ch[:, :, :], expert_no[:, :].unsqueeze(1).to_broadcast([P, TOP_K, E]),
                top_if[:, :].unsqueeze(2).to_broadcast([P, TOP_K, E]), ALU.is_equal),
                t_f, t_expert_no, *c_left)
            routing[b, j] = (cs, ch, t_c, t_w)

        def count_before(b, j):
            i = b * NJ + j
            cs, ch, t_c, t_w = routing[b, j]
            PE.wait(t_c, t_before, *last.get("ps_count", ()))
            for k in range(TOP_K):
                make = lambda k=k: M.matmul(ps_count[:, 0:E], before[:, :], ch[:, k, :],
                                            start=(i == 0 and k == 0), stop=(k == TOP_K - 1),
                                            skip_group_check=(i > 0))
                mm = PE.do(make) if k == TOP_K - 1 else PE.quiet(make)
            routing[b, j] = (cs, ch, mm, t_w)

        def place_choices(b, j):
            i = b * NJ + j
            cs, ch, mm, t_w = routing[b, j]
            t_p = DVE.do(lambda: V.tensor_tensor(
                placed[:, :, :], ch[:, :, :], ps_count[:, 0:E].unsqueeze(1).to_broadcast([P, TOP_K, E]), ALU.mult),
                mm, *last.get("placed", ()))
            last["ps_count"] = (t_p,)
            t_pl = DVE.do(lambda: V.tensor_reduce(place[:, :], placed[:, :, :], AX.X, ALU.add), t_p, *last.get("place", ()))
            last["placed"] = (t_pl,)
            t_slot = DVE.do(lambda: V.scalar_tensor_tensor(
                out=slot_of[:, i, :], in0=place[:, :], scalar=float(E), in1=top_if[:, :], op0=ALU.mult, op1=ALU.add), t_pl)
            last["place"] = last["top_if"] = (t_slot,)
            routing[b, j] = (cs, ch, t_p, t_slot, t_w)

        def count_rest(b, j):
            cs, ch, t_p, t_slot, t_w = routing[b, j]
            PE.wait(t_p)
            for k in range(TOP_K):
                make = lambda k=k: M.matmul(ps_count[:, 0:E], not_before[:, :], ch[:, k, :],
                                            start=False, stop=(k == TOP_K - 1), skip_group_check=True)
                mm = PE.do(make) if k == TOP_K - 1 else PE.quiet(make)
            chosen_ring.leave(cs, t_p, mm)

        def scatter_choices(b, j):
            i = b * NJ + j
            cs, ch, t_p, t_slot, t_w = routing[b, j]
            for k in range(TOP_K):
                scattered.append(POOL.dma(lambda k=k: G.indirect_dma_start(
                    table_dram, bass.IndirectOffsetOnAxis(slot_of[:, i, k:k + 1], 0), pairs[:, i, k, :], None,
                    bounds_check=SLOTS - 1, oob_is_err=False), scatter_lane, t_slot, t_w, table_empty))

        w_lane = lanes("w_lane", NW)
        w_ready, w_left = {}, {}

        def load_expert(e, *ticks):
            s = e % NW
            SP.dma(lambda: Y.dma_start(wgu_buf[s][:, :, :], w_gu[e].rearrange("(k p) n -> p k n", p=P)), w_lane[s],
                   w_left.get(e - NW), *ticks)
            w_ready[e] = SP.dma(lambda: Y.dma_start(wdn_buf[s][:, :, :],
                                                    w_down[e].rearrange("(h p) n -> p h n", p=IH)), w_lane[s])

        OUT = {(2, 1): (1, 0), (3, 0): (1, 1), (3, 2): (1, 2), (0, 1): (2, 3)}
        DIVIDE = {(1, 0): 0, (1, 1): 1, (1, 2): 2, (2, 0): 3}

        def mix_piece(it, c, at):
            if (c, at) in DIVIDE and 0 <= it - 1 < NB:
                divide(it - 1, DIVIDE[c, at])
            if (c, at) in OUT:
                back, j = OUT[c, at]
                if 0 <= it - back < NB:
                    out_project(it - back, j)
            if c == 0 and 0 <= it - 1 < NB:
                if at == 0:
                    sum_heads(it - 1)
                if at == 1:
                    turn_rden(it - 1)

        def attention_step(it, c):
            working = it < NB
            n = it * KC + c - 2 * KC
            tile = (n // KC, n % KC) if 0 <= n < NT else None
            n -= 1
            before_tile = (n // KC, n % KC) if 0 <= n < NT else None
            if working:
                project_k(it, c)
            if before_tile:
                choose(*before_tile)
            while x1_open:
                store_x1()
            mix_piece(it, c, 0)
            if before_tile:
                count_before(*before_tile)
            if working:
                project_v(it, c)
                scan_k(it, c)
            if before_tile:
                place_choices(*before_tile)
            if tile:
                turn(*tile)
            if working:
                scan_kv(it, c)
            mix_piece(it, c, 1)
            if working:
                project_q(it, c)
            if before_tile:
                count_rest(*before_tile)
                scatter_choices(*before_tile)
            if tile:
                score_experts(*tile)
            mix_piece(it, c, 2)
            if it + 1 < NB:
                split_x(it + 1, c)
                ahead = (it + 1) * KC + c + 2
                if ahead < NB * KC:
                    load_x(ahead // KC, ahead % KC)
            if 0 <= it - 1 < NB:
                for j in {1: (0, 1), 2: (2,), 3: (3,)}.get(c, ()):
                    load_xres(it - 1, j)

        for it in range(NB):
            for c in range(KC):
                attention_step(it, c)
        load_expert(0)
        load_expert(1)

        projected = (x_left[NB - 1], (DVE.sem, DVE.count), (SCA.sem, SCA.count))
        shared_lane = lanes("shared_lane", 1)[0]
        shared_w = {}

        def split_shared(name, src, hi, lo, n):
            view = x1t_stage[:, :, :].rearrange("p k t -> p (k t)")[:, 0:n * src.shape[2]].rearrange("p (k t) -> p k t", k=n)
            t = SP.dma(lambda: Y.dma_start(view, src), shared_lane, *projected, *last.get("x1t_stage", ()))
            SCA.wait(*projected)
            DVE.wait(*projected)
            last["x1t_stage"] = shared_w[name] = split(hi[:, :, :], lo[:, :, :], view, t)

        ps_up, ps_down = Ring(banks[0:2]), Ring(banks[2:3])
        x1t_split, hid_ready, rows_ready = {}, {}, {}

        def shared_load(b):
            src = x1t_dram.rearrange("(k p) t -> p k t", p=P)[:, :, b * BT:(b + 1) * BT]
            t = SP.dma(lambda: Y.dma_start(x1t_stage[:, :, :], src), shared_lane,
                       *[x1t_stored[b, j] for j in range(NJ)], *last["x1t_stage"])
            x1t_split[b] = t

        def shared_split(b):
            ticks = []
            for k in range(KC):
                ticks += split(x1t_hi[:, k, :], x1t_lo[:, k, :], x1t_stage[:, k, :], x1t_split[b], *last.get("x1t_hi", ()))
            last["x1t_stage"] = x1t_split[b] = tuple(ticks)

        def shared_up(b, c):
            cols = slice(c * P, (c + 1) * P)
            gs, psg, g_left = ps_up.take()
            products = []
            for k in range(KC):
                products += three(sg_hi[:, k, cols], sg_lo[:, k, cols], x1t_hi[:, k, :], x1t_lo[:, k, :])
            mm_g = group(psg[:, :], products, *shared_w["g"], *x1t_split[b], *g_left)
            t = SCA.do(lambda: S.activation(tanh_s[:, :], psg[:, :], ACT.Tanh, scale=0.5), mm_g, *last.get("tanh_s", ()))
            t_silu = DVE.do(lambda: V.scalar_tensor_tensor(out=silu_s[:, :], in0=tanh_s[:, :], scalar=1.0, in1=psg[:, :],
                                                           op0=ALU.add, op1=ALU.mult), t, *last.get("silu_s", ()))
            last["tanh_s"] = (t_silu,)
            ps_up.leave(gs, t_silu)
            yield
            us, psu, u_left = ps_up.take()
            products = []
            for k in range(KC):
                products += three(su_hi[:, k, cols], su_lo[:, k, cols], x1t_hi[:, k, :], x1t_lo[:, k, :])
            mm_u = group(psu[:, :], products, *shared_w["u"], *u_left)
            if c == SC - 1:
                last["x1t_hi"] = (mm_u,)
            t = DVE.do(lambda: V.scalar_tensor_tensor(out=hid_s[:, :], in0=silu_s[:, :], scalar=0.5, in1=psu[:, :],
                                                      op0=ALU.mult, op1=ALU.mult), t_silu, mm_u, *last.get("hid_s", ()))
            last["silu_s"] = (t,)
            ps_up.leave(us, t)
            hid_ready[b, c] = split(hid_hi[:, c, :], hid_lo[:, c, :], hid_s[:, :], t, *last.get("hid_hi", ()))
            last["hid_s"] = hid_ready[b, c]
            yield

        def shared_down(b, j):
            tok = slice(j * P, (j + 1) * P)
            slot, ps, left = ps_down.take()
            products = []
            for c in range(SC):
                products += three(hid_hi[:, c, tok], hid_lo[:, c, tok], sd_hi[:, c, :], sd_lo[:, c, :])
            mm = group(ps[:, :], products, *shared_w["d"], *[t for c in range(SC) for t in hid_ready[b, c]], *left)
            if j == NJ - 1:
                last["hid_hi"] = (mm,)
            if b < NB - TAIL:
                t = SCA.do(lambda: S.copy(shared_rows[b][:, j, :], ps[:, :]), mm)
                ps_down.leave(slot, t)
                rows_ready[b, j] = (shared_rows[b][:, j, :], t, None)
            else:
                rows_ready[b, j] = (ps[:, :], mm, slot)

        def shared_units():
            shared_load(0)
            for b in range(NB):
                shared_split(b)
                if b + 1 < NB:
                    shared_load(b + 1)
                for c in range(SC):
                    yield from shared_up(b, c)
                for j in range(NJ):
                    shared_down(b, j)
                    if b >= NB - TAIL:
                        finish_tile(b, j)
                    if j % 2:
                        yield
        UNITS = 2 * SC + NJ // 2

        fin_lane, fin_out = lanes("fin_lane", 2), lanes("fin_out", 2)
        fin_in, written, normed = {}, {}, {}

        def finish_load(b):
            src = acc_dram[b * BT:(b + 1) * BT, :].rearrange("(j p) d -> p j d", p=P)
            fin_in[b] = SP.dma(lambda: Y.dma_start(fin_sb[b % 2][:, :, :], src), fin_lane[b % 2],
                               added[0], w_left[E - 1], w_left[E - 2], written.get(b - 2))

        def finish_tile(b, j):
            if b not in fin_in:
                finish_load(b)
            z = fin_sb[b % 2][:, j, :]
            rows, t_rows, slot = rows_ready[b, j]
            t = DVE.do(lambda: V.tensor_tensor(z, rows, z, ALU.add), fin_in[b], t_rows)
            if slot is not None:
                ps_down.leave(slot, t)
            normed[b, j] = norm(z, t)()
            if j == NJ - 1:
                dst = out[b * BT:(b + 1) * BT, :].rearrange("(j p) d -> p j d", p=P)
                written[b] = SP.dma(lambda: Y.dma_start(dst, fin_sb[b % 2][:, :, :]), fin_out[b % 2],
                                    *[normed[b, i] for i in range(NJ)])

        split_shared("g", sg_t.rearrange("(k p) n -> p k n", p=P), sg_hi, sg_lo, KC)
        units = shared_units()
        for c in range(KC):
            attention_step(NB, c)
            if c == 0:
                split_shared("u", su_t.rearrange("(k p) n -> p k n", p=P), su_hi, su_lo, KC)
            if c == 1:
                split_shared("d", sd_t.rearrange("(k p) n -> p k n", p=P), sd_hi, sd_lo, SC)
        done_units = 0
        for c in range(KC):
            attention_step(NB + 1, c)
        attention_step(NB + 2, 0)
        attention_end = tuple((q.sem, q.count) for q in (PE, DVE, SCA, POOL))

        table_in = load("table_in", table_sb[:, :, :], table_v, scattered[-1], table_empty)
        ps_xg, ps_gu, ps_ht, ps_eo = Ring(banks[3:4]), Ring(banks[4:6]), Ring(banks[6:7]), Ring(banks[7:8])
        xg_ring, xgt_ring, eo_ring = Ring(xg), Ring(xgt), Ring(eo)
        hid_e_ring, hid_et_ring = Ring(hid_e), Ring(hid_et)
        xg_lane, add_lane = lanes("xg_lane", len(xg)), Lane(sem("add_lane"))
        xg_ready, xgt_ready, hid_e_ready, added = {}, {}, {}, [None]

        def gather(e):
            slot, buf, left = xg_ring.take()
            t = POOL.dma(lambda: G.indirect_dma_start(
                buf[:, :], None, x1_dram, bass.IndirectOffsetOnAxis(table_sb[:, e, 0:1], 0),
                bounds_check=T - 1, oob_is_err=False), xg_lane[slot], table_in, *left)
            xg_ready[e] = (slot, buf, t)

        def turn_rows(e):
            gs, buf, t_g = xg_ready[e]
            ps_slot, ps, left = ps_xg.take()
            PE.wait(t_g, *left)
            for k in range(KC):
                make = lambda k=k: M.transpose(ps[:, k * P:(k + 1) * P], buf[:, k * P:(k + 1) * P], ident[:, :])
                mm = PE.do(make) if k == KC - 1 else PE.quiet(make)
            xg_ring.leave(gs, mm)
            ts, xt, t_left = xgt_ring.take()
            t = DVE.do(lambda: V.tensor_copy(xt[:, :, :], ps[:, :].rearrange("p (k s) -> p k s", k=KC)), mm, *t_left)
            ps_xg.leave(ps_slot, t)
            xgt_ready[e] = (ts, xt, t)

        def gate_up(e):
            ts, xt, t_x = xgt_ready[e]
            slot, ps, left = ps_gu.take()
            w = wgu_buf[e % NW]
            mm = group(ps[:, 0:GU], [(xt[:, k, :], w[:, k, :]) for k in range(KC)], t_x, w_ready[e], *left)
            xgt_ring.leave(ts, mm)
            t = SCA.do(lambda: S.activation(tanh_e[:, :], ps[:, 0:I], ACT.Tanh, scale=0.5), mm, *last.get("tanh_e", ()))
            t = DVE.do(lambda: V.scalar_tensor_tensor(out=silu_e[:, :], in0=tanh_e[:, :], scalar=1.0, in1=ps[:, 0:I],
                                                      op0=ALU.add, op1=ALU.mult), t, *last.get("silu_e", ()))
            last["tanh_e"] = (t,)
            hs, h, h_left = hid_e_ring.take()
            t = DVE.do(lambda: V.scalar_tensor_tensor(out=h[:, :], in0=silu_e[:, :], scalar=0.5, in1=ps[:, I:GU],
                                                      op0=ALU.mult, op1=ALU.mult), t, *h_left)
            last["silu_e"] = (t,)
            ps_gu.leave(slot, t)
            hid_e_ready[e] = (hs, h, t)

        def turn_hidden(e):
            hs, h, t_h = hid_e_ready[e]
            slot, ps, left = ps_ht.take()
            PE.wait(t_h, *left)
            for k in range(2):
                make = lambda k=k: M.transpose(ps[0:IH, k * P:(k + 1) * P], h[:, k * IH:(k + 1) * IH], ident[:, :])
                mm = PE.do(make) if k else PE.quiet(make)
            hid_e_ring.leave(hs, mm)
            ts, ht, t_left = hid_et_ring.take()
            t = SCA.do(lambda: S.copy(ht[:, :, :], ps[0:IH, 0:2 * P].rearrange("p (h s) -> p h s", h=2)), mm, *t_left)
            ps_ht.leave(slot, t)
            return ts, ht, t

        def down(e, ts, ht, t):
            slot, ps, left = ps_eo.take()
            w = wdn_buf[e % NW]
            mm = group(ps[:, :], [(ht[:, k, :], w[:, k, :]) for k in range(2)], t, *left)
            hid_et_ring.leave(ts, mm)
            w_left[e] = mm
            es, eob, e_left = eo_ring.take()
            t = SCA.do(lambda: S.activation(eob[:, :], ps[:, :], ACT.Copy, scale=table_sb[:, e, 1:2].bitcast(F32)),
                       mm, table_in, *e_left)
            ps_eo.leave(slot, t)
            return es, eob, t

        def add_rows(e, es, eob, t):
            a = POOL.dma(lambda: G.indirect_dma_start(
                acc_dram, bass.IndirectOffsetOnAxis(table_sb[:, e, 0:1], 0), eob[:, :], None,
                bounds_check=T - 1, oob_is_err=False, compute_op=ALU.add), add_lane, t, added[0])
            added[0] = a
            eo_ring.leave(es, a)

        for q in (SP, PE, DVE, SCA, POOL):
            q.wait(*attention_end)
        POOL.wait(*x1_stored)
        for e in range(2, NW):
            load_expert(e)
        for _ in range(UNITS):
            next(units)
            done_units += 1
        AHEAD = len(xg)
        for e in range(AHEAD - 1):
            gather(e)
        turn_rows(0)
        pending = turned = None
        total = (NB - TAIL) * UNITS
        for e in range(E):
            if e + AHEAD - 1 < E:
                gather(e + AHEAD - 1)
            gate_up(e)
            if e + 1 < E:
                turn_rows(e + 1)
            if pending:
                add_rows(*pending)
            if turned:
                pending = (e - 1, *down(e - 1, *turned))
                if e - 1 + NW < E:
                    load_expert(e - 1 + NW)
            while done_units < total and (done_units - UNITS) * E < (e + 1) * (total - UNITS):
                next(units)
                done_units += 1
            turned = turn_hidden(e)
        add_rows(*pending)
        add_rows(E - 1, *down(E - 1, *turned))

        for b in range(NB - TAIL):
            finish_load(b) if b not in fin_in else None
            for j in range(NJ):
                finish_tile(b, j)
        for _ in units:
            pass
        SP.wait(*[written[b] for b in range(NB - 2, NB)])

        block = ctx.enter_context(nc.Block())

        @block.sync
        def _(eng):
            SP.flush(eng)

        @block.scalar
        def _(eng):
            SCA.flush(eng)

        @block.vector
        def _(eng):
            DVE.flush(eng)

        @block.gpsimd
        def _(eng):
            POOL.flush(eng)

        @block.tensor
        def _(eng):
            PE.flush(eng)


def kernel(**inputs):
    import concourse.bacc as bacc
    from concourse.bass_utils import run_bass_kernel_spmd

    a = {name: np.asarray(v) for name, v in inputs.items()}
    x = a["L0_attn_x"]
    B, T, D = x.shape
    rows = x.reshape(B * T, D)
    decay = np.repeat(a["L0_attn_decay_param"], D // HEADS).reshape(D // P, P).T
    arrays = {
        "x": rows, "x_t": rows.T, "w_qkv": a["L0_attn_w_qkv"], "w_out": a["L0_attn_w_out"],
        "decay_param": decay, "gate_t": a["L0_ffn_gate_w"].T,
        "w_gu": a["L0_ffn_gate_up_proj"], "w_down": a["L0_ffn_down_proj"],
        "sg_t": a["L0_ffn_shared_gate_w"].T, "su_t": a["L0_ffn_shared_up_w"].T, "sd_t": a["L0_ffn_shared_down_w"].T,
    }
    arrays = {name: np.ascontiguousarray(v) for name, v in arrays.items()}
    nc = bacc.Bacc("TRN2", target_bir_lowering=False, num_devices=1)
    aps = {name: nc.dram_tensor(name, v.shape, mybir.dt.from_np(v.dtype), kind="ExternalInput").ap()
           for name, v in arrays.items()}
    out = nc.dram_tensor("out", (B * T, D), F32, kind="ExternalOutput").ap()
    build(nc, out=out, **aps)
    r = run_bass_kernel_spmd(nc, [arrays], core_ids=[0])
    return r.results[0]["out"].reshape(B, T, D)
```

```python
from contextlib import ExitStack

import numpy as np

import concourse.bass as bass
from concourse import mybir

F32 = mybir.dt.float32
F32R = mybir.dt.float32r
BF16 = mybir.dt.bfloat16
U32 = mybir.dt.uint32
ALU = mybir.AluOpType
ACT = mybir.ActivationFunctionType
AX = mybir.AxisListType

P = 128
HEADS = 16
TOP_K = 6
CAP = 128
EPS_NORM = 1e-5
EPS_DEN = 1e-6


class Queue:

    def __init__(self, name, sem):
        self.name, self.sem, self.count, self.items, self.seen = name, sem, 0, [], {}

    def wait(self, *ticks):
        for tick in ticks:
            if tick is None:
                continue
            sem, value = tick
            if self.seen.get(id(sem), 0) < value:
                self.seen[id(sem)] = value
                self.items.append((None, sem, value))

    def do(self, make, *ticks):
        self.wait(*ticks)
        self.count += 1
        self.items.append((make, self.sem, 1))
        return self.sem, self.count

    def quiet(self, make, *ticks):
        self.wait(*ticks)
        self.items.append((make, None, 0))

    def dma(self, make, lane, *ticks):
        self.wait(*ticks)
        lane.count += 16
        self.items.append((make, lane.sem, 16))
        return lane.sem, lane.count

    def flush(self, engine):
        for make, sem, value in self.items:
            if make is None:
                engine.wait_ge(sem, value)
            elif sem is None:
                make()
            else:
                make().then_inc(sem, value)


class Lane:

    def __init__(self, sem):
        self.sem, self.count = sem, 0


class Ring:

    def __init__(self, buffers):
        self.buffers, self.left, self.n = buffers, [() for _ in buffers], 0

    def take(self):
        slot = self.n % len(self.buffers)
        self.n += 1
        left, self.left[slot] = self.left[slot], None
        assert left is not None, "the slot's last use has not been left"
        return slot, self.buffers[slot], left

    def leave(self, slot, *ticks):
        self.left[slot] = ticks


class Map:

    def __init__(self, nc, start, end):
        self.nc, self.at, self.end = nc, start, end

    def place(self, name, shape, dt=F32):
        size = int(np.prod(shape[1:])) * (2 if dt == BF16 else 4)
        offset = self.at
        self.at += (size + 31) // 32 * 32
        assert self.at <= self.end, (name, self.at, self.end)
        return self.nc.alloc_sbuf_tensor_at(name, shape, dt, offset=offset)


def build(nc, x, x_t, w_qkv, w_out, decay_param, gate_t, w_gu, w_down, sg_t, su_t, sd_t, out):
    T, D = x.shape
    E, _, GU = w_gu.shape
    I = GU // 2
    SI = sg_t.shape[1]
    BT = 512
    NB = T // BT
    NJ = BT // P
    NT = T // P
    KC = D // P
    SC = SI // P
    IH = I // 2
    SLOTS = E * CAP
    HW = D // HEADS
    TAIL = 4
    NW = 5
    assert SC < NJ and KC == NJ and SI == GU and NB % 2 == 0

    x1_dram = nc.dram_tensor("x1_rows", (T, D), F32, kind="Internal").ap()
    x1t_dram = nc.dram_tensor("x1_turned", (D, T), F32, kind="Internal").ap()
    acc_dram = nc.dram_tensor("acc_rows", (T, D), F32, kind="Internal").ap()
    table_dram = nc.dram_tensor("slot_table", (SLOTS, 2), U32, kind="Internal").ap()

    start, end = (nc.sbuf_base + 31) // 32 * 32, nc.sbuf_usable_end
    both = Map(nc, start, end)
    ident = both.place("ident", [P, P])
    minus_half = both.place("minus_half", [P, 1])
    table_sb = both.place("table_sb", [P, E, 2], U32)
    stats = both.place("stats", [P, 6])
    mv = [both.place(f"mv{i}", [P, 2]) for i in range(2)]
    rstd = [both.place(f"rstd{i}", [P, 1]) for i in range(2)]
    wgu_buf = [both.place(f"wgu{i}", [P, KC, GU]) for i in range(2)]
    wdn_buf = [both.place(f"wdn{i}", [IH, 2, D]) for i in range(2)]

    att = Map(nc, both.at, end)
    wqkv_hi = att.place("wqkv_hi", [P, 3 * KC, KC, P], F32R)
    wqkv_lo = att.place("wqkv_lo", [P, 3 * KC, KC, P], F32R)
    x_stage = [att.place(f"x_stage{i}", [P, BT]) for i in range(2)]
    x_hi = [att.place(f"x_hi{i}", [P, KC, BT], F32R) for i in range(2)]
    x_lo = [att.place(f"x_lo{i}", [P, KC, BT], F32R) for i in range(2)]
    projected_end = att.at
    e_sb = [att.place(f"e{i}", [P, BT]) for i in range(2)]
    relu_sb = [att.place("relu", [P, BT])]
    phi_k = att.place("phi_k", [P, BT])
    kv = att.place("kv", [P, BT])
    run_k = att.place("run_k", [P, BT])
    run_kv = att.place("run_kv", [P, BT])
    phi_q = att.place("phi_q", [P, BT])
    qk = [att.place(f"qk{i}", [P, BT]) for i in range(KC + 1)]
    wout_hi = att.place("wout_hi", [P, KC, D], F32R)
    wout_lo = att.place("wout_lo", [P, KC, D], F32R)
    gate_sb = att.place("gate_sb", [P, KC, E])
    before = att.place("before", [P, P], BF16)
    not_before = att.place("not_before", [P, P], BF16)
    ones = att.place("ones", [P, P], BF16)
    head_sum = att.place("head_sum", [P, KC, HEADS])
    head_send = att.place("head_send", [HEADS, KC, P], F32R)
    expert_no = att.place("expert_no", [P, E], BF16)
    decay = att.place("decay", [P, KC])
    xres = [att.place(f"xres{i}", [P, D]) for i in range(2)]
    state = att.place("state", [P, KC, 2])
    num = [att.place(f"num{i}", [P, BT]) for i in range(KC + 2)]
    att_hi = att.place("att_hi", [P, KC, BT], F32R)
    att_lo = att.place("att_lo", [P, KC, BT], F32R)
    rden = att.place("rden", [P, NJ, HEADS])
    rden_hi = att.place("rden_hi", [HEADS, BT], F32R)
    rden_lo = att.place("rden_lo", [HEADS, BT], F32R)
    neg_max = att.place("neg_max", [P, 1])
    e_route = att.place("e_route", [P, E])
    e_sum = att.place("e_sum", [P, 1])
    r_sum = att.place("r_sum", [P, 1])
    score = att.place("score", [P, E])
    top_v = att.place("top_v", [P, 8])
    top_i = att.place("top_i", [P, 8], U32)
    top_if = att.place("top_if", [P, TOP_K])
    chosen = [att.place(f"chosen{i}", [P, TOP_K, E], BF16) for i in range(2)]
    placed = att.place("placed", [P, TOP_K, E])
    place = att.place("place", [P, TOP_K])
    kept_from = att.at
    x1_sb = [att.place(f"x1_{i}", [P, D]) for i in range(NJ)]
    x1t_sb = [att.place(f"x1t{i}", [P, KC, P]) for i in range(2)]
    slot_of = att.place("slot_of", [P, NT, TOP_K], U32)
    pairs = att.place("pairs", [P, NT, TOP_K, 2], U32)

    chunk = 3 * KC * P * 4
    half = KC * BT * 4
    hi_at, lo_at = both.at, both.at + KC * chunk
    x_at = lo_at + KC * chunk + 2 * BT * 4
    sg_hi = Map(nc, hi_at, hi_at + chunk).place("sg_hi", [P, KC, SI], F32R)
    sg_lo = Map(nc, lo_at, lo_at + chunk).place("sg_lo", [P, KC, SI], F32R)
    su_hi = Map(nc, hi_at + chunk, hi_at + 2 * chunk).place("su_hi", [P, KC, SI], F32R)
    su_lo = Map(nc, lo_at + chunk, lo_at + 2 * chunk).place("su_lo", [P, KC, SI], F32R)
    sd_hi = Map(nc, hi_at + 2 * chunk, hi_at + 3 * chunk).place("sd_hi", [P, SC, D], F32R)
    sd_lo = Map(nc, lo_at + 2 * chunk, lo_at + 3 * chunk).place("sd_lo", [P, SC, D], F32R)
    x1t_stage = Map(nc, x_at, x_at + half).place("x1t_stage", [P, KC, BT])
    x1t_hi = Map(nc, x_at + 2 * half, x_at + 3 * half).place("x1t_hi", [P, KC, BT], F32R)
    x1t_lo = Map(nc, x_at + half, x_at + 2 * half).place("x1t_lo", [P, KC, BT], F32R)
    hid_hi = Map(nc, x_at + 3 * half, x_at + 4 * half).place("hid_hi", [P, SC, BT], F32R)
    hid_lo = Map(nc, hi_at + 3 * chunk, lo_at).place("hid_lo", [P, SC, BT], F32R)
    rest = Map(nc, lo_at + 3 * chunk, lo_at + 4 * chunk)
    tanh_s = rest.place("tanh_s", [P, BT])
    silu_s = rest.place("silu_s", [P, BT])
    hid_s = rest.place("hid_s", [P, BT])
    late = Map(nc, projected_end, kept_from)
    shared_rows = [late.place(f"shared_rows{b}", [P, NJ, D]) for b in range(NB - TAIL)]
    late_weights_at = late.at
    wgu_buf += [late.place(f"wgu{i}", [P, KC, GU]) for i in range(2, NW)]
    wdn_buf += [late.place(f"wdn{i}", [IH, 2, D]) for i in range(2, NW)]
    xg = [late.place(f"xg{i}", [P, D]) for i in range(3)]
    xgt = [late.place(f"xgt{i}", [P, KC, P]) for i in range(2)]
    eo = [late.place(f"eo{i}", [P, D]) for i in range(3)]
    tanh_e = late.place("tanh_e", [P, I])
    silu_e = late.place("silu_e", [P, I])
    hid_e = [late.place(f"hid_e{i}", [P, I]) for i in range(2)]
    hid_et = [late.place(f"hid_et{i}", [IH, 2, P]) for i in range(2)]
    fin_map = Map(nc, both.at - 2 * 4 * (KC * GU + 2 * D), both.at)
    fin_sb = [fin_map.place(f"fin{i}", [P, NJ, D]) for i in range(2)]
    fin_map = Map(nc, late_weights_at, late_weights_at + (NW - 2) * 4 * (KC * GU + 2 * D))
    fin_sb += [fin_map.place(f"fin{i}", [P, NJ, D]) for i in range(2, NW)]

    ctx = ExitStack()
    with ctx:
        def sem(name):
            return ctx.enter_context(nc.semaphore(name))

        banks = [ctx.enter_context(nc.psum_tensor(f"bank{i}", [P, 512], F32)) for i in range(8)]

        PE = Queue("PE", sem("pe"))
        DVE = Queue("DVE", sem("dve"))
        SCA = Queue("ACT", sem("act"))
        POOL = Queue("POOL", sem("pool"))
        SP = Queue("SP", None)
        V, S, G, M, Y = nc.vector, nc.scalar, nc.gpsimd, nc.tensor, nc.sync
        last = {}

        def lanes(name, n):
            return [Lane(sem(f"{name}{i}")) for i in range(n)]

        def load(name, dst, src, *ticks):
            return SP.dma(lambda: Y.dma_start(dst, src), Lane(sem(f"ld_{name}")), *ticks)

        def split(hi, lo, src, t_src, *left):
            t_hi = SCA.do(lambda: S.copy(hi, src), t_src, *left)
            t_lo = DVE.do(lambda: V.tensor_tensor(lo, src, hi.bitcast(F32), ALU.subtract), t_hi, t_src, *left)
            return t_hi, t_lo

        def group(out_ap, products, *ticks):
            n = len(products)
            for i, (a, b) in enumerate(products):
                make = lambda a=a, b=b, i=i: M.matmul(out_ap, a, b, start=(i == 0), stop=(i == n - 1))
                PE.wait(*(ticks if i == 0 else ()))
                t = PE.do(make) if i == n - 1 else PE.quiet(make)
            return t

        def three(a_hi, a_lo, b_hi, b_lo):
            return [(a_hi, b_hi), (a_hi, b_lo), (a_lo, b_hi)]

        t = POOL.do(lambda: G.memset(ident[:, :], 0.0))
        t_ident = POOL.do(lambda: G.affine_select(
            out=ident[:, :], in_=ident[:, :], compare_op=ALU.not_equal, fill=1.0, base=0,
            pattern=[[-1, P]], channel_multiplier=1), t)
        t_ones = POOL.do(lambda: G.memset(ones[:, :], 1.0))
        t_before = POOL.do(lambda: G.affine_select(
            out=before[:, :], in_=ones[:, :], compare_op=ALU.is_ge, fill=0.0, base=-1,
            pattern=[[1, P]], channel_multiplier=-1), t_ones)
        t_before = POOL.do(lambda: G.affine_select(
            out=not_before[:, :], in_=ones[:, :], compare_op=ALU.is_ge, fill=0.0, base=0,
            pattern=[[-1, P]], channel_multiplier=1), t_ones)

        per_chunk = P // HW

        def head_mask(buf, rows_are_channels):
            t = POOL.do(lambda: G.memset(buf, 1.0))
            for sign, base in ((1, 0), (-1, HW - 1)):
                if rows_are_channels:
                    pattern, mult = [[sign * HW * per_chunk, KC], [-sign * HW, HEADS]], sign
                else:
                    pattern, mult = [[sign * HW * per_chunk, KC], [sign, P]], -sign * HW
                t = POOL.do(lambda pattern=pattern, mult=mult, base=base: G.affine_select(
                    out=buf, in_=buf, compare_op=ALU.is_ge, fill=0.0, base=base,
                    pattern=pattern, channel_multiplier=mult), t)
            return t

        t_sum = head_mask(head_sum[:, :, :], True)
        mask_f = kv[0:HEADS, :].rearrange("p (k c) -> p k c", k=KC)
        t = head_mask(mask_f, False)
        t_send = POOL.do(lambda: G.tensor_copy(head_send[:, :, :], mask_f), t)
        last["kv"] = (t_send,)
        t_expert_no = POOL.do(lambda: G.iota(expert_no[:, :], pattern=[[1, E]], base=0, channel_multiplier=0,
                                             allow_small_or_imprecise_dtypes=True))
        t_half = POOL.do(lambda: G.memset(minus_half[:, :], -0.5))
        t_token = POOL.do(lambda: G.iota(pairs[:, :, :, 0], pattern=[[P, NT], [0, TOP_K]], base=0,
                                         channel_multiplier=1))
        t1 = POOL.do(lambda: G.iota(table_sb[:, :, 0], pattern=[[0, E]], base=T, channel_multiplier=0))
        t2 = POOL.do(lambda: G.iota(table_sb[:, :, 1], pattern=[[0, E]], base=0, channel_multiplier=0))
        table_v = table_dram.rearrange("(s e) w -> s e w", e=E)

        num_ring = Ring(num)
        stage_lane = lanes("stage_lane", len(num))
        wq_v = w_qkv.rearrange("(k p) n -> p k n", p=P)
        wqkv_ready, wout_ready = {}, {}

        def stage_weights(key, src, hi, lo, ready):
            slot, buf, left = num_ring.take()
            shape = buf[:, :]
            view = shape if len(hi.shape) == 2 else shape.rearrange("p (k n) -> p k n", k=KC)
            t = SP.dma(lambda: Y.dma_start(view, src), stage_lane[slot], *left)
            ticks = split(hi, lo, view, t)
            num_ring.leave(slot, *ticks)
            ready[key] = ticks

        x_ring, x_lane = Ring(x_stage), lanes("x_lane", 2)
        x_staged, x_ready, x_left = {}, {}, {}

        def load_x(b, k):
            slot, buf, left = x_ring.take()
            src = x_t[k * P:(k + 1) * P, b * BT:(b + 1) * BT]
            x_staged[b, k] = slot, buf, SP.dma(lambda: Y.dma_start(buf[:, :], src), x_lane[slot], *left)

        def split_x(b, k):
            i = b % 2
            slot, buf, t = x_staged[b, k]
            x_ready[b, k] = split(x_hi[i][:, k, :], x_lo[i][:, k, :], buf[:, :], t, x_left.get(b - 2))
            x_ring.leave(slot, *x_ready[b, k])

        decay_in = load("decay", decay[:, :], decay_param)
        load_x(0, 0)
        load_x(0, 1)
        PARTS = (1, 2, 0)
        for c in range(KC):
            for n, part in enumerate(PARTS):
                cols = slice(part * D + c * P, part * D + (c + 1) * P)
                i = 3 * c + n
                stage_weights((c, n), wq_v[:, :, cols], wqkv_hi[:, i, :, :], wqkv_lo[:, i, :, :], wqkv_ready)
                if i == 0:
                    for k in range(KC):
                        split_x(0, k)
                        if k + 2 < KC:
                            load_x(0, k + 2)
        load_x(1, 0)
        load_x(1, 1)
        for c in range(KC):
            stage_weights(c, w_out[c * P:(c + 1) * P, :], wout_hi[:, c, :], wout_lo[:, c, :], wout_ready)
        gate_in = load("gate", gate_sb[:, :, :], gate_t.rearrange("(k p) n -> p k n", p=P))
        table_empty = load("table_empty", table_v, table_sb[:, :, :], t1, t2)
        t = SCA.do(lambda: S.activation(decay[:, :], decay[:, :], ACT.Exp, scale=-1.0), decay_in)
        t = DVE.do(lambda: V.tensor_scalar(decay[:, :], decay[:, :], 1.0, None, ALU.add), t)
        t_decay = DVE.do(lambda: V.reciprocal(decay[:, :], decay[:, :]), t)
        t_state = DVE.do(lambda: V.memset(state[:, :, :], 0.0))

        ps_proj = Ring(banks[0:3])
        e_ring, relu_ring, qk_ring = Ring(e_sb), Ring(relu_sb), Ring(qk)
        num_ready, qk_ready, state_tick = {}, {}, {}

        def project_group(b, c, n):
            slot, ps, left = ps_proj.take()
            xh, xl = x_hi[b % 2], x_lo[b % 2]
            i = 3 * c + n
            products = []
            for k in range(KC):
                products += three(wqkv_hi[:, i, k, :], wqkv_lo[:, i, k, :], xh[:, k, :], xl[:, k, :])
            ready = [t for k in range(KC) for t in x_ready[b, k]] if (c, n) == (0, 0) else []
            mm = group(ps[:, :], products, *ready, *wqkv_ready[c, n], *left)
            return slot, ps, mm

        def feature_map(dst, n, b, c, *dst_left):
            slot, ps, mm = project_group(b, c, n)
            es, e, e_left = e_ring.take()
            rs, r, r_left = relu_ring.take()
            te = SCA.do(lambda: S.activation(e[:, :], ps[:, :], ACT.Exp), mm, *e_left)
            tr = SCA.do(lambda: S.activation(r[:, :], ps[:, :], ACT.Relu), *r_left)
            ps_proj.leave(slot, tr)
            t = DVE.do(lambda: V.scalar_tensor_tensor(out=dst[:, :], in0=e[:, :], scalar=1.0, in1=r[:, :],
                                                      op0=ALU.min, op1=ALU.add), te, tr, *dst_left)
            e_ring.leave(es, t)
            relu_ring.leave(rs, t)
            return t, mm

        projected = {}
        running = {}

        def project_k(b, c):
            running["k"], _ = feature_map(phi_k, 0, b, c, *last.get("phi_k", ()))

        def scan_k(b, c):
            dec = decay[:, c:c + 1].to_broadcast([P, BT])
            running["rk"] = DVE.do(lambda: V.tensor_tensor_scan(
                out=run_k[:, :], data0=dec, data1=phi_k[:, :], initial=state[:, c, 0:1],
                op0=ALU.mult, op1=ALU.add), running["k"], t_decay, t_state, state_tick.get(c), *last.get("run_k", ()))

        def project_v(b, c):
            running["v"] = project_group(b, c, 1)

        def scan_kv(b, c):
            slot, ps, mm_v = running["v"]
            dec = decay[:, c:c + 1].to_broadcast([P, BT])
            t_kv = DVE.do(lambda: V.tensor_tensor(kv[:, :], phi_k[:, :], ps[:, :], ALU.mult),
                          mm_v, *last.get("kv", ()))
            ps_proj.leave(slot, t_kv)
            last["phi_k"] = (running["rk"], t_kv)
            running["rkv"] = DVE.do(lambda: V.tensor_tensor_scan(
                out=run_kv[:, :], data0=dec, data1=kv[:, :], initial=state[:, c, 1:2],
                op0=ALU.mult, op1=ALU.add), t_kv, *last.get("run_kv", ()))
            last["kv"] = (running["rkv"],)

        def project_q(b, c):
            t_q, mm_q = feature_map(phi_q, 2, b, c, *last.get("phi_q", ()))
            projected[b, c] = mm_q
            if c == KC - 1:
                x_left[b] = mm_q
            t_sk = SCA.do(lambda: S.copy(state[:, c, 0:1], run_k[:, BT - 1:BT]), running["rk"])
            t_skv = SCA.do(lambda: S.copy(state[:, c, 1:2], run_kv[:, BT - 1:BT]), running["rkv"])
            state_tick[c] = t_skv
            qs, qkb, q_left = qk_ring.take()
            t_qk = DVE.do(lambda: V.tensor_tensor(qkb[:, :], phi_q[:, :], run_k[:, :], ALU.mult), t_q, *q_left)
            ns, nm, n_left = num_ring.take()
            t_num = POOL.do(lambda: G.tensor_tensor(nm[:, :], phi_q[:, :], run_kv[:, :], ALU.mult),
                            t_q, running["rkv"], *n_left)
            last["run_k"] = (t_qk, t_sk)
            last["run_kv"] = (t_num, t_skv)
            last["phi_q"] = (t_qk, t_num)
            qk_ready[b, c] = (qs, qkb, t_qk)
            num_ready[b, c] = (ns, nm, t_num)

        ps_send, ps_small = Ring(banks[6:7]), Ring(banks[5:6])
        den_tick, att_ready, att_left, att_open = {}, {}, {}, []

        def sum_heads(b, tiles):
            slot, ps, left = ps_small.take()
            for j in tiles:
                mm = group(ps[:, j * HEADS:(j + 1) * HEADS],
                           [(qk_ready[b, c][1][:, j * P:(j + 1) * P], head_sum[:, c, :]) for c in range(KC)],
                           *[qk_ready[b, c][2] for c in range(KC)], t_sum, *left)
            if j == NJ - 1:
                for c in range(KC):
                    qk_ring.leave(qk_ready[b, c][0], mm)
            cols = slice(tiles[0] * HEADS, (j + 1) * HEADS)
            flat = rden[:, :, :].rearrange("p j h -> p (j h)")[:, cols]
            t = DVE.do(lambda: V.tensor_scalar(flat, ps[:, cols], EPS_DEN, None, ALU.max),
                       mm, *last.get("rden", ()))
            ps_small.leave(slot, t)
            den_tick[b] = DVE.do(lambda: V.reciprocal(flat, flat), t)

        def turn_rden(b):
            slot, ps, left = ps_send.take()
            PE.wait(den_tick[b], t_ident, *left)
            for j in range(NJ):
                make = lambda j=j: M.transpose(ps[0:HEADS, j * P:(j + 1) * P], rden[:, j, :], ident[:, :])
                mm = PE.do(make) if j == NJ - 1 else PE.quiet(make)
            last["rden"] = (mm,)
            den_tick[b] = split(rden_hi[:, :], rden_lo[:, :], ps[0:HEADS, :], mm, *last.get("rden_hi", ()))
            ps_send.leave(slot, *den_tick[b])

        def divide(b, c):
            slot, ps, left = ps_send.take()
            mm = group(ps[:, :], [(head_send[:, c, :], rden_hi[:, :]), (head_send[:, c, :], rden_lo[:, :])],
                       t_send, *den_tick[b], *left)
            ns, nm, t_num = num_ready[b, c]
            t = DVE.do(lambda: V.tensor_tensor(nm[:, :], nm[:, :], ps[:, :], ALU.mult), mm, t_num)
            ps_send.leave(slot, t)
            last["rden_hi"] = (mm,)
            att_open.append((b, c, ns, nm, t))

        def split_att():
            b, c, ns, nm, t = att_open.pop(0)
            att_ready[b, c] = split(att_hi[:, c, :], att_lo[:, c, :], nm[:, :], t, att_left.get(b - 1))
            num_ring.leave(ns, *att_ready[b, c])

        xres_ring, xres_lane, xres_ready = Ring(xres), lanes("xres_lane", len(xres)), {}

        def load_xres(b, j):
            slot, buf, left = xres_ring.take()
            row = b * BT + j * P
            t = SP.dma(lambda: Y.dma_start(buf[:, :], x[row:row + P, :]), xres_lane[slot], *left)
            xres_ready[b, j] = (slot, buf, t)

        norms = [0]

        def norm(buf, t_src):
            i = norms[0] % 2
            norms[0] += 1
            t = DVE.do(lambda: V.bn_stats(stats[:, :], buf), t_src, *last.get("stats", ()))
            t_mv = DVE.do(lambda: V.bn_aggr(mv[i][:, :], stats[:, :]), t, *last.get(f"mv{i}", ()))
            last["stats"] = (t_mv,)
            t = POOL.do(lambda: G.tensor_scalar(rstd[i][:, :], mv[i][:, 1:2], EPS_NORM, None, ALU.add),
                        t_mv, *last.get(f"mv{i}", ()))
            t_r = POOL.do(lambda: G.tensor_tensor(rstd[i][:, :], rstd[i][:, :], minus_half[:, :], ALU.pow), t, t_half)

            def apply():
                t = DVE.do(lambda: V.tensor_scalar(buf, buf, mv[i][:, 0:1], rstd[i][:, 0:1],
                                                   ALU.subtract, ALU.mult), t_r, t_mv)
                last[f"mv{i}"] = (t,)
                return t
            return apply

        ps_rows_a = Ring(banks[4:5])
        x1_ring, x1_lane = Ring(x1_sb), lanes("x1_lane", len(x1_sb))
        acc_lane = lanes("acc_lane", len(x1_sb))
        x1_ready, x1_stored, x1_open = {}, [], []

        def out_project(b, j):
            slot, ps, left = ps_rows_a.take()
            tok = slice(j * P, (j + 1) * P)
            products = []
            for k in range(KC):
                products += three(att_hi[:, k, tok], att_lo[:, k, tok], wout_hi[:, k, :], wout_lo[:, k, :])
            ready = [t for c in range(KC) for t in (*att_ready[b, c], *wout_ready[c])]
            mm = group(ps[:, :], products, *ready, *left)
            if j == NJ - 1:
                att_left[b] = mm
            xs, xr, t_x = xres_ready[b, j]
            x1s, x1, x1_left = x1_ring.take()
            t = DVE.do(lambda: V.tensor_tensor(x1[:, :], ps[:, :], xr[:, :], ALU.add), mm, t_x, *x1_left)
            ps_rows_a.leave(slot, t)
            xres_ring.leave(xs, t)
            x1_open.append((b, j, x1s, x1, norm(x1[:, :], t)))

        def store_x1():
            b, j, x1s, x1, apply = x1_open.pop(0)
            t = apply()
            row = b * BT + j * P
            w1 = SP.dma(lambda: Y.dma_start(x1_dram[row:row + P, :], x1[:, :]), x1_lane[x1s], t)
            w2 = SP.dma(lambda: Y.dma_start(acc_dram[row:row + P, :], x1[:, :]), acc_lane[x1s], t)
            x1_stored.extend((w1, w2))
            x1_ready[b, j] = (x1s, x1, t, w1, w2)

        ps_turn, ps_count = Ring(banks[3:4]), banks[7]
        x1t_ring, x1t_lane, x1t_stored = Ring(x1t_sb), lanes("x1t_lane", len(x1t_sb)), {}
        chosen_ring = Ring(chosen)
        scatter_lane = Lane(sem("scatter_lane"))
        scattered = []

        turned, routing = {}, {}

        def turn(b, j):
            slot, ps, left = ps_turn.take()
            x1s, x1, t_x1, w1, w2 = x1_ready[b, j]
            PE.wait(t_x1, t_ident, *left)
            for k in range(KC):
                make = lambda k=k: M.transpose(ps[:, k * P:(k + 1) * P], x1[:, k * P:(k + 1) * P], ident[:, :])
                mm = PE.do(make) if k == KC - 1 else PE.quiet(make)
            x1_ring.leave(x1s, mm, w1, w2)
            ts, x1t, t_left = x1t_ring.take()
            t = SCA.do(lambda: S.copy(x1t[:, :, :], ps[:, :].rearrange("p (k t) -> p k t", k=KC)), mm, *t_left)
            ps_turn.leave(slot, t)
            col = b * BT + j * P
            dst = x1t_dram.rearrange("(k p) t -> p k t", p=P)[:, :, col:col + P]
            w = SP.dma(lambda: Y.dma_start(dst, x1t[:, :, :]), x1t_lane[ts], t)
            x1t_stored[b, j] = w
            turned[b, j] = (ts, x1t, t, w)

        def score_experts(b, j):
            ts, x1t, t, w = turned[b, j]
            slot, logits, left = ps_small.take()
            mm = group(logits[:, 0:E], [(x1t[:, k, :], gate_sb[:, k, :]) for k in range(KC)], t, gate_in, *left)
            x1t_ring.leave(ts, mm, w)
            t = DVE.do(lambda: V.tensor_reduce(neg_max[:, :], logits[:, 0:E], AX.X, ALU.max, negate=True),
                       mm, *last.get("neg_max", ()))
            t_e = SCA.do(lambda: S.activation(e_route[:, :], logits[:, 0:E], ACT.Exp, bias=neg_max[:, 0:1],
                                              accum_out=e_sum[:, :]), t, *last.get("e_route", ()))
            last["neg_max"] = (t_e,)
            ps_small.leave(slot, t_e)
            routing[b, j] = t_e

        def choose(b, j):
            i = b * NJ + j
            t_e = routing[b, j]
            t = DVE.do(lambda: V.reciprocal(r_sum[:, :], e_sum[:, :]), t_e, *last.get("r_sum", ()))
            t_s = DVE.do(lambda: V.tensor_scalar(score[:, :], e_route[:, :], r_sum[:, 0:1], None, ALU.mult),
                         t, *last.get("score", ()))
            last["e_route"] = last["r_sum"] = (t_s,)
            t_v = DVE.do(lambda: V.max(top_v[:, :], score[:, :]), t_s, *last.get("top_v", ()))
            t_i = DVE.do(lambda: V.max_index(top_i[:, :], top_v[:, :], score[:, :]), t_v, *last.get("top_i", ()))
            last["score"] = (t_i,)
            t_w = SCA.do(lambda: S.copy(pairs[:, i, :, 1].bitcast(F32), top_v[:, 0:TOP_K]), t_v, t_token)
            last["top_v"] = (t_w, t_i)
            t_f = DVE.do(lambda: V.tensor_copy(top_if[:, :], top_i[:, 0:TOP_K]), t_i, *last.get("top_if", ()))
            last["top_i"] = (t_f,)
            cs, ch, c_left = chosen_ring.take()
            t_c = DVE.do(lambda: V.tensor_tensor(
                ch[:, :, :], expert_no[:, :].unsqueeze(1).to_broadcast([P, TOP_K, E]),
                top_if[:, :].unsqueeze(2).to_broadcast([P, TOP_K, E]), ALU.is_equal),
                t_f, t_expert_no, *c_left)
            routing[b, j] = (cs, ch, t_c, t_w)

        def count_before(b, j):
            i = b * NJ + j
            cs, ch, t_c, t_w = routing[b, j]
            PE.wait(t_c, t_before, *last.get("ps_count", ()))
            for k in range(TOP_K):
                make = lambda k=k: M.matmul(ps_count[:, 0:E], before[:, :], ch[:, k, :],
                                            start=(i == 0 and k == 0), stop=(k == TOP_K - 1),
                                            skip_group_check=(i > 0))
                mm = PE.do(make) if k == TOP_K - 1 else PE.quiet(make)
            routing[b, j] = (cs, ch, mm, t_w)

        def place_choices(b, j):
            i = b * NJ + j
            cs, ch, mm, t_w = routing[b, j]
            t_p = DVE.do(lambda: V.tensor_tensor(
                placed[:, :, :], ch[:, :, :], ps_count[:, 0:E].unsqueeze(1).to_broadcast([P, TOP_K, E]), ALU.mult),
                mm, *last.get("placed", ()))
            last["ps_count"] = (t_p,)
            t_pl = DVE.do(lambda: V.tensor_reduce(place[:, :], placed[:, :, :], AX.X, ALU.add), t_p, *last.get("place", ()))
            last["placed"] = (t_pl,)
            t_slot = DVE.do(lambda: V.scalar_tensor_tensor(
                out=slot_of[:, i, :], in0=place[:, :], scalar=float(E), in1=top_if[:, :], op0=ALU.mult, op1=ALU.add), t_pl)
            last["place"] = last["top_if"] = (t_slot,)
            routing[b, j] = (cs, ch, t_p, t_slot, t_w)

        def count_rest(b, j):
            cs, ch, t_p, t_slot, t_w = routing[b, j]
            PE.wait(t_p)
            for k in range(TOP_K):
                make = lambda k=k: M.matmul(ps_count[:, 0:E], not_before[:, :], ch[:, k, :],
                                            start=False, stop=(k == TOP_K - 1), skip_group_check=True)
                mm = PE.do(make) if k == TOP_K - 1 else PE.quiet(make)
            chosen_ring.leave(cs, t_p, mm)

        def scatter_choices(b, j):
            i = b * NJ + j
            cs, ch, t_p, t_slot, t_w = routing[b, j]
            for k in range(TOP_K):
                scattered.append(POOL.dma(lambda k=k: G.indirect_dma_start(
                    table_dram, bass.IndirectOffsetOnAxis(slot_of[:, i, k:k + 1], 0), pairs[:, i, k, :], None,
                    bounds_check=SLOTS - 1, oob_is_err=False), scatter_lane, t_slot, t_w, table_empty))

        w_lane = lanes("w_lane", NW)
        w_ready, w_left = {}, {}

        def load_expert(e, *ticks):
            s = e % NW
            SP.dma(lambda: Y.dma_start(wgu_buf[s][:, :, :], w_gu[e].rearrange("(k p) n -> p k n", p=P)), w_lane[s],
                   w_left.get(e - NW), *ticks)
            w_ready[e] = SP.dma(lambda: Y.dma_start(wdn_buf[s][:, :, :],
                                                    w_down[e].rearrange("(h p) n -> p h n", p=IH)), w_lane[s])

        shared_lane = lanes("shared_lane", 1)[0]
        shared_w = {}

        def load_shared(name, src):
            n = src.shape[1]
            view = x1t_stage[:, :, :].rearrange("p k t -> p (k t)")[:, 0:n * src.shape[2]].rearrange("p (k t) -> p k t", k=n)
            t = SP.dma(lambda: Y.dma_start(view, src), shared_lane, x_left[NB - 2], *last.get("x1t_stage", ()))
            shared_w[name] = view, t

        def split_shared(name, hi, lo, c):
            view, t = shared_w[name]
            last["x1t_stage"] = shared_w[name] = split(hi[:, :, :], lo[:, :, :], view, t, projected[NB - 1, c])

        x1t_split, hid_ready, rows_ready = {}, {}, {}

        def shared_load(b):
            src = x1t_dram.rearrange("(k p) t -> p k t", p=P)[:, :, b * BT:(b + 1) * BT]
            t = SP.dma(lambda: Y.dma_start(x1t_stage[:, :, :], src), shared_lane,
                       *[x1t_stored[b, j] for j in range(NJ)], *last["x1t_stage"])
            x1t_split[b] = t

        def shared_split(b):
            ticks = []
            SCA.wait(x_left[NB - 1])
            DVE.wait(x_left[NB - 1])
            for k in range(KC):
                ticks += split(x1t_hi[:, k, :], x1t_lo[:, k, :], x1t_stage[:, k, :], x1t_split[b], *last.get("x1t_hi", ()))
            last["x1t_stage"] = x1t_split[b] = tuple(ticks)

        def shared_up(b, c):
            cols = slice(c * P, (c + 1) * P)
            gs, psg, g_left = ps_proj.take()
            products = []
            for k in range(KC):
                products += three(sg_hi[:, k, cols], sg_lo[:, k, cols], x1t_hi[:, k, :], x1t_lo[:, k, :])
            mm_g = group(psg[:, :], products, *shared_w["g"], *x1t_split[b], *g_left)
            t = SCA.do(lambda: S.activation(tanh_s[:, :], psg[:, :], ACT.Tanh, scale=0.5), mm_g, *last.get("tanh_s", ()))
            t_silu = DVE.do(lambda: V.scalar_tensor_tensor(out=silu_s[:, :], in0=tanh_s[:, :], scalar=1.0, in1=psg[:, :],
                                                           op0=ALU.add, op1=ALU.mult), t, *last.get("silu_s", ()))
            last["tanh_s"] = (t_silu,)
            ps_proj.leave(gs, t_silu)
            yield
            us, psu, u_left = ps_proj.take()
            products = []
            for k in range(KC):
                products += three(su_hi[:, k, cols], su_lo[:, k, cols], x1t_hi[:, k, :], x1t_lo[:, k, :])
            mm_u = group(psu[:, :], products, *shared_w["u"], *u_left)
            if c == SC - 1:
                last["x1t_hi"] = (mm_u,)
            t = DVE.do(lambda: V.scalar_tensor_tensor(out=hid_s[:, :], in0=silu_s[:, :], scalar=0.5, in1=psu[:, :],
                                                      op0=ALU.mult, op1=ALU.mult), t_silu, mm_u, *last.get("hid_s", ()))
            last["silu_s"] = (t,)
            ps_proj.leave(us, t)
            hid_ready[b, c] = split(hid_hi[:, c, :], hid_lo[:, c, :], hid_s[:, :], t, *last.get("hid_hi", ()))
            last["hid_s"] = hid_ready[b, c]
            yield

        def shared_down(b, j):
            tok = slice(j * P, (j + 1) * P)
            slot, ps, left = ps_proj.take()
            products = []
            for c in range(SC):
                products += three(hid_hi[:, c, tok], hid_lo[:, c, tok], sd_hi[:, c, :], sd_lo[:, c, :])
            mm = group(ps[:, :], products, *shared_w["d"], *[t for c in range(SC) for t in hid_ready[b, c]], *left)
            if j == NJ - 1:
                last["hid_hi"] = (mm,)
            if b < NB - TAIL:
                t = SCA.do(lambda: S.copy(shared_rows[b][:, j, :], ps[:, :]), mm, *rows_free)
                ps_proj.leave(slot, t)
                rows_ready[b, j] = (shared_rows[b][:, j, :], t, None)
            else:
                rows_ready[b, j] = (ps[:, :], mm, slot)

        def shared_units():
            shared_split(0)
            for b in range(NB):
                if b + 1 < NB:
                    shared_load(b + 1)
                for c in range(SC):
                    yield from shared_up(b, c)
                if b + 1 < NB:
                    shared_split(b + 1)
                for j in range(NJ):
                    shared_down(b, j)
                    if b >= NB - TAIL:
                        finish_tile(b, j)
                    if j % 2:
                        yield
        UNITS = 2 * SC + NJ // 2
        units = shared_units()
        done_units = [0]

        def fill():
            next(units)
            done_units[0] += 1

        OUT = {(2, 2): (1, 0), (3, 0): (1, 1), (3, 2): (1, 2), (0, 1): (2, 3)}
        DIVIDE = {(1, 0): 0, (1, 1): 1, (1, 2): 2, (2, 0): 3}

        def mix_piece(it, c, at):
            if (c, at) in DIVIDE and 0 <= it - 1 < NB:
                divide(it - 1, DIVIDE[c, at])
            if (c, at) in OUT:
                back, j = OUT[c, at]
                if 0 <= it - back < NB:
                    out_project(it - back, j)
            if c == 0 and 0 <= it - 1 < NB:
                if at < 2:
                    sum_heads(it - 1, range(at * NJ // 2, (at + 1) * NJ // 2))

        def attention_step(it, c):
            working = it < NB
            n = it * KC + c - 2 * KC
            tile = (n // KC, n % KC) if 0 <= n < NT else None
            n -= 1
            before_tile = (n // KC, n % KC) if 0 <= n < NT else None
            if before_tile:
                choose(*before_tile)
            if it + 1 < NB:
                split_x(it + 1, c)
                ahead = (it + 1) * KC + c + 2
                if ahead < NB * KC:
                    load_x(ahead // KC, ahead % KC)
            if working:
                project_k(it, c)
            else:
                fill()
            while att_open:
                split_att()
            mix_piece(it, c, 0)
            if working:
                project_v(it, c)
            if before_tile:
                count_before(*before_tile)
            if working:
                scan_k(it, c)
            if before_tile:
                place_choices(*before_tile)
            while att_open:
                split_att()
            if tile:
                turn(*tile)
            if working:
                scan_kv(it, c)
            while x1_open:
                store_x1()
            mix_piece(it, c, 1)
            if working:
                project_q(it, c)
            else:
                fill()
            while att_open:
                split_att()
            if c == 0 and 0 <= it - 1 < NB:
                turn_rden(it - 1)
            if before_tile:
                count_rest(*before_tile)
            if tile:
                score_experts(*tile)
            mix_piece(it, c, 2)
            if before_tile:
                scatter_choices(*before_tile)
            if 0 <= it - 1 < NB:
                for j in {1: (0, 1), 2: (2,), 3: (3,)}.get(c, ()):
                    load_xres(it - 1, j)

        fin_lane, fin_out = lanes("fin_lane", NW), lanes("fin_out", NJ // 2 * NW)
        fin_buf, added, written, written_of, open_norms, to_load = {}, [None], [], {}, [], []
        fin_ring = Ring(fin_sb)

        def finish_load(b):
            slot, buf, left = fin_ring.take()
            src = acc_dram[b * BT:(b + 1) * BT, :].rearrange("(j p) d -> p j d", p=P)
            t = SP.dma(lambda: Y.dma_start(buf[:, :, :], src), fin_lane[slot], added[0], w_left[E - 1], *left)
            fin_buf[b] = slot, buf, t

        def finish_tile(b, j):
            slot, buf, t_in = fin_buf[b]
            z = buf[:, j, :]
            rows, t_rows, rows_slot = rows_ready[b, j]
            t = DVE.do(lambda: V.tensor_tensor(z, rows, z, ALU.add), t_in, t_rows)
            if rows_slot is not None:
                ps_proj.leave(rows_slot, t)
            open_norms.append((b, j, norm(z, t)))
            if len(open_norms) > 1:
                finish_norm()

        def finish_norm():
            b, j, apply = open_norms.pop(0)
            slot, buf, t_in = fin_buf[b]
            t = apply()
            if j % 2:
                dst = out[b * BT + (j - 1) * P:b * BT + (j + 1) * P, :].rearrange("(j p) d -> p j d", p=P)
                w = SP.dma(lambda: Y.dma_start(dst, buf[:, j - 1:j + 1, :]), fin_out[NJ // 2 * slot + j // 2], t)
                written.append(w)
                written_of.setdefault(b, []).append(w)
                if j == NJ - 1:
                    fin_ring.leave(slot, *written_of.pop(b), w)
                    if to_load:
                        finish_load(to_load.pop(0))

        shared_src = {"g": sg_t.rearrange("(k p) n -> p k n", p=P), "u": su_t.rearrange("(k p) n -> p k n", p=P),
                      "d": sd_t.rearrange("(k p) n -> p k n", p=P)}
        for it in range(NB):
            for c in range(KC):
                attention_step(it, c)
                if it == NB - 1:
                    if c == 0:
                        load_shared("g", shared_src["g"])
                    if c == 1:
                        split_shared("g", sg_hi, sg_lo, 0)
                        load_shared("u", shared_src["u"])
                    if c == 2:
                        split_shared("u", su_hi, su_lo, 1)
                        load_shared("d", shared_src["d"])
                    if c == 3:
                        split_shared("d", sd_hi, sd_lo, 2)
                        shared_load(0)
        load_expert(0)
        load_expert(1)
        rows_free = tuple((q.sem, q.count) for q in (DVE, SCA, POOL))
        for it in (NB, NB + 1):
            for c in range(KC):
                attention_step(it, c)
        attention_step(NB + 2, 0)
        attention_end = tuple((q.sem, q.count) for q in (PE, DVE, SCA, POOL))
        rows_free = attention_end

        table_in = load("table_in", table_sb[:, :, :], table_v, scattered[-1], table_empty)
        ps_xg, ps_gu, ps_ht, ps_eo = Ring(banks[3:4]), Ring(banks[4:6]), Ring(banks[6:7]), Ring(banks[7:8])
        xg_ring, xgt_ring, eo_ring = Ring(xg), Ring(xgt), Ring(eo)
        hid_e_ring, hid_et_ring = Ring(hid_e), Ring(hid_et)
        xg_lane, add_lane = lanes("xg_lane", len(xg)), Lane(sem("add_lane"))
        xg_ready, xgt_ready, hid_e_ready = {}, {}, {}

        def gather(e):
            slot, buf, left = xg_ring.take()
            t = POOL.dma(lambda: G.indirect_dma_start(
                buf[:, :], None, x1_dram, bass.IndirectOffsetOnAxis(table_sb[:, e, 0:1], 0),
                bounds_check=T - 1, oob_is_err=False), xg_lane[slot], table_in, *left)
            xg_ready[e] = (slot, buf, t)

        def turn_rows(e):
            gs, buf, t_g = xg_ready[e]
            ps_slot, ps, left = ps_xg.take()
            PE.wait(t_g, *left)
            for k in range(KC):
                make = lambda k=k: M.transpose(ps[:, k * P:(k + 1) * P], buf[:, k * P:(k + 1) * P], ident[:, :])
                mm = PE.do(make) if k == KC - 1 else PE.quiet(make)
            xg_ring.leave(gs, mm)
            ts, xt, t_left = xgt_ring.take()
            t = DVE.do(lambda: V.tensor_copy(xt[:, :, :], ps[:, :].rearrange("p (k s) -> p k s", k=KC)), mm, *t_left)
            ps_xg.leave(ps_slot, t)
            xgt_ready[e] = (ts, xt, t)

        def gate_up(e):
            ts, xt, t_x = xgt_ready[e]
            slot, ps, left = ps_gu.take()
            w = wgu_buf[e % NW]
            mm = group(ps[:, 0:GU], [(xt[:, k, :], w[:, k, :]) for k in range(KC)], t_x, w_ready[e], *left)
            xgt_ring.leave(ts, mm)
            t = SCA.do(lambda: S.activation(tanh_e[:, :], ps[:, 0:I], ACT.Tanh, scale=0.5), mm, *last.get("tanh_e", ()))
            t = DVE.do(lambda: V.scalar_tensor_tensor(out=silu_e[:, :], in0=tanh_e[:, :], scalar=1.0, in1=ps[:, 0:I],
                                                      op0=ALU.add, op1=ALU.mult), t, *last.get("silu_e", ()))
            last["tanh_e"] = (t,)
            hs, h, h_left = hid_e_ring.take()
            t = DVE.do(lambda: V.scalar_tensor_tensor(out=h[:, :], in0=silu_e[:, :], scalar=0.5, in1=ps[:, I:GU],
                                                      op0=ALU.mult, op1=ALU.mult), t, *h_left)
            last["silu_e"] = (t,)
            ps_gu.leave(slot, t)
            hid_e_ready[e] = (hs, h, t)

        def turn_hidden(e):
            hs, h, t_h = hid_e_ready[e]
            slot, ps, left = ps_ht.take()
            PE.wait(t_h, *left)
            for k in range(2):
                make = lambda k=k: M.transpose(ps[0:IH, k * P:(k + 1) * P], h[:, k * IH:(k + 1) * IH], ident[:, :])
                mm = PE.do(make) if k else PE.quiet(make)
            hid_e_ring.leave(hs, mm)
            ts, ht, t_left = hid_et_ring.take()
            t = SCA.do(lambda: S.copy(ht[:, :, :], ps[0:IH, 0:2 * P].rearrange("p (h s) -> p h s", h=2)), mm, *t_left)
            ps_ht.leave(slot, t)
            return ts, ht, t

        def down(e, ts, ht, t):
            slot, ps, left = ps_eo.take()
            w = wdn_buf[e % NW]
            mm = group(ps[:, :], [(ht[:, k, :], w[:, k, :]) for k in range(2)], t, *left)
            hid_et_ring.leave(ts, mm)
            w_left[e] = mm
            es, eob, e_left = eo_ring.take()
            t = SCA.do(lambda: S.activation(eob[:, :], ps[:, :], ACT.Copy, scale=table_sb[:, e, 1:2].bitcast(F32)),
                       mm, table_in, *e_left)
            ps_eo.leave(slot, t)
            return es, eob, t

        def add_rows(e, es, eob, t):
            a = POOL.dma(lambda: G.indirect_dma_start(
                acc_dram, bass.IndirectOffsetOnAxis(table_sb[:, e, 0:1], 0), eob[:, :], None,
                bounds_check=T - 1, oob_is_err=False, compute_op=ALU.add), add_lane, t, added[0])
            added[0] = a
            eo_ring.leave(es, a)

        for q in (SP, PE, DVE, SCA, POOL):
            q.wait(*attention_end)
        POOL.wait(*x1_stored)
        for e in range(2, NW):
            load_expert(e)
        for _ in range(UNITS):
            fill()
        AHEAD = len(xg)
        for e in range(AHEAD - 1):
            gather(e)
        turn_rows(0)
        pending = turned = None
        total, before_units = (NB - TAIL) * UNITS, done_units[0]
        for e in range(E):
            if e + AHEAD - 1 < E:
                gather(e + AHEAD - 1)
            gate_up(e)
            if e + 1 < E:
                turn_rows(e + 1)
            if pending:
                add_rows(*pending)
            if turned:
                pending = (e - 1, *down(e - 1, *turned))
                if e - 1 + NW < E:
                    load_expert(e - 1 + NW)
            while done_units[0] < total and (done_units[0] - before_units) * E < (e + 1) * (total - before_units):
                fill()
            turned = turn_hidden(e)
        add_rows(*pending)
        add_rows(E - 1, *down(E - 1, *turned))

        early = [(b, j) for b in range(NB - TAIL) for j in range(NJ)]
        order = [b for i in range(TAIL) for b in (NB - TAIL + i, i)]
        assert TAIL * 2 == NB
        for b in order[0:NW]:
            finish_load(b)
        to_load.extend(order[NW:])
        for i in range(TAIL * UNITS):
            fill()
            if i % 2:
                finish_tile(*early.pop(0))
        while open_norms:
            finish_norm()
        SP.wait(*written)

        block = ctx.enter_context(nc.Block())

        @block.sync
        def _(eng):
            SP.flush(eng)

        @block.scalar
        def _(eng):
            SCA.flush(eng)

        @block.vector
        def _(eng):
            DVE.flush(eng)

        @block.gpsimd
        def _(eng):
            POOL.flush(eng)

        @block.tensor
        def _(eng):
            PE.flush(eng)


def kernel(**inputs):
    import concourse.bacc as bacc
    from concourse.bass_utils import run_bass_kernel_spmd

    a = {name: np.asarray(v) for name, v in inputs.items()}
    x = a["L0_attn_x"]
    B, T, D = x.shape
    rows = x.reshape(B * T, D)
    decay = np.repeat(a["L0_attn_decay_param"], D // HEADS).reshape(D // P, P).T
    arrays = {
        "x": rows, "x_t": rows.T, "w_qkv": a["L0_attn_w_qkv"], "w_out": a["L0_attn_w_out"],
        "decay_param": decay, "gate_t": a["L0_ffn_gate_w"].T,
        "w_gu": a["L0_ffn_gate_up_proj"], "w_down": a["L0_ffn_down_proj"],
        "sg_t": a["L0_ffn_shared_gate_w"].T, "su_t": a["L0_ffn_shared_up_w"].T, "sd_t": a["L0_ffn_shared_down_w"].T,
    }
    arrays = {name: np.ascontiguousarray(v) for name, v in arrays.items()}
    nc = bacc.Bacc("TRN2", target_bir_lowering=False, num_devices=1)
    aps = {name: nc.dram_tensor(name, v.shape, mybir.dt.from_np(v.dtype), kind="ExternalInput").ap()
           for name, v in arrays.items()}
    out = nc.dram_tensor("out", (B * T, D), F32, kind="ExternalOutput").ap()
    build(nc, out=out, **aps)
    r = run_bass_kernel_spmd(nc, [arrays], core_ids=[0])
    return r.results[0]["out"].reshape(B, T, D)
```

```python
from contextlib import ExitStack

import numpy as np

import concourse.bass as bass
from concourse import mybir

F32 = mybir.dt.float32
F32R = mybir.dt.float32r
BF16 = mybir.dt.bfloat16
U32 = mybir.dt.uint32
ALU = mybir.AluOpType
ACT = mybir.ActivationFunctionType
AX = mybir.AxisListType

P = 128
HEADS = 16
TOP_K = 6
CAP = 128
EPS_NORM = 1e-5
EPS_DEN = 1e-6


class Queue:

    def __init__(self, name, sem):
        self.name, self.sem, self.count, self.items, self.seen = name, sem, 0, [], {}

    def wait(self, *ticks):
        for tick in ticks:
            if tick is None:
                continue
            sem, value = tick
            if self.seen.get(id(sem), 0) < value:
                self.seen[id(sem)] = value
                self.items.append((None, sem, value))

    def do(self, make, *ticks):
        self.wait(*ticks)
        self.count += 1
        self.items.append((make, self.sem, 1))
        return self.sem, self.count

    def quiet(self, make, *ticks):
        self.wait(*ticks)
        self.items.append((make, None, 0))

    def dma(self, make, lane, *ticks):
        self.wait(*ticks)
        lane.count += 16
        self.items.append((make, lane.sem, 16))
        return lane.sem, lane.count

    def flush(self, engine):
        for make, sem, value in self.items:
            if make is None:
                engine.wait_ge(sem, value)
            elif sem is None:
                make()
            else:
                make().then_inc(sem, value)


class Lane:

    def __init__(self, sem):
        self.sem, self.count = sem, 0


class Ring:

    def __init__(self, buffers):
        self.buffers, self.left, self.n = buffers, [() for _ in buffers], 0

    def take(self):
        slot = self.n % len(self.buffers)
        self.n += 1
        left, self.left[slot] = self.left[slot], None
        assert left is not None, "the slot's last use has not been left"
        return slot, self.buffers[slot], left

    def leave(self, slot, *ticks):
        self.left[slot] = ticks


class Map:

    def __init__(self, nc, start, end):
        self.nc, self.at, self.end = nc, start, end

    def place(self, name, shape, dt=F32):
        size = int(np.prod(shape[1:])) * (2 if dt == BF16 else 4)
        offset = self.at
        self.at += (size + 31) // 32 * 32
        assert self.at <= self.end, (name, self.at, self.end)
        return self.nc.alloc_sbuf_tensor_at(name, shape, dt, offset=offset)


def build(nc, x, x_t, w_qkv, w_out, decay_param, gate_t, w_gu, w_down, sg_t, su_t, sd_t, out):
    T, D = x.shape
    E, _, GU = w_gu.shape
    I = GU // 2
    SI = sg_t.shape[1]
    BT = 512
    NB = T // BT
    NJ = BT // P
    NT = T // P
    KC = D // P
    SC = SI // P
    IH = I // 2
    SLOTS = E * CAP
    HW = D // HEADS
    TAIL = 3
    NG, ND = 3, 4
    assert SC < NJ and KC == NJ and SI == GU and NB % 2 == 0

    x1_dram = nc.dram_tensor("x1_rows", (T, D), F32, kind="Internal").ap()
    x1t_dram = nc.dram_tensor("x1_turned", (D, T), F32, kind="Internal").ap()
    acc_dram = nc.dram_tensor("acc_rows", (T, D), F32, kind="Internal").ap()
    table_dram = nc.dram_tensor("slot_table", (SLOTS, 2), U32, kind="Internal").ap()

    start, end = (nc.sbuf_base + 31) // 32 * 32, nc.sbuf_usable_end
    both = Map(nc, start, end)
    ident = both.place("ident", [P, P])
    minus_half = both.place("minus_half", [P, 1])
    table_sb = both.place("table_sb", [P, E, 2], U32)
    stats = both.place("stats", [P, 6])
    mv = [both.place(f"mv{i}", [P, 2]) for i in range(4)]
    rstd = [both.place(f"rstd{i}", [P, 1]) for i in range(4)]
    shift = [both.place(f"shift{i}", [P, 1]) for i in range(4)]
    wgu_buf = [both.place(f"wgu{i}", [P, KC, GU]) for i in range(2)]
    wdn_buf = [both.place(f"wdn{i}", [IH, 2, D]) for i in range(2)]

    att = Map(nc, both.at, end)
    wqkv_hi = att.place("wqkv_hi", [P, 3 * KC, KC, P], F32R)
    wqkv_lo = att.place("wqkv_lo", [P, 3 * KC, KC, P], F32R)
    x_stage = [att.place(f"x_stage{i}", [P, BT]) for i in range(2)]
    x_hi = [att.place(f"x_hi{i}", [P, KC, BT], F32R) for i in range(2)]
    x_lo = [att.place(f"x_lo{i}", [P, KC, BT], F32R) for i in range(2)]
    projected_end = att.at
    e_sb = [att.place(f"e{i}", [P, BT]) for i in range(2)]
    relu_sb = [att.place("relu", [P, BT])]
    phi_k = att.place("phi_k", [P, BT])
    kv = att.place("kv", [P, BT])
    run_k = att.place("run_k", [P, BT])
    run_kv = att.place("run_kv", [P, BT])
    phi_q = att.place("phi_q", [P, BT])
    qk = [att.place(f"qk{i}", [P, BT]) for i in range(KC + 1)]
    wout_hi = att.place("wout_hi", [P, KC, D], F32R)
    wout_lo = att.place("wout_lo", [P, KC, D], F32R)
    gate_sb = att.place("gate_sb", [P, KC, E])
    before = att.place("before", [P, P], BF16)
    not_before = att.place("not_before", [P, P], BF16)
    ones = att.place("ones", [P, P], BF16)
    head_sum = att.place("head_sum", [P, KC, HEADS])
    head_send = att.place("head_send", [HEADS, KC, P], F32R)
    expert_no = att.place("expert_no", [P, E], BF16)
    decay = att.place("decay", [P, KC])
    xres = [att.place(f"xres{i}", [P, D]) for i in range(2)]
    state = att.place("state", [P, KC, 2])
    num = [att.place(f"num{i}", [P, BT]) for i in range(KC + 2)]
    att_hi = att.place("att_hi", [P, KC, BT], F32R)
    att_lo = att.place("att_lo", [P, KC, BT], F32R)
    rden = att.place("rden", [P, NJ, HEADS])
    rden_hi = att.place("rden_hi", [HEADS, BT], F32R)
    rden_lo = att.place("rden_lo", [HEADS, BT], F32R)
    neg_max = att.place("neg_max", [P, 1])
    e_route = att.place("e_route", [P, E])
    e_sum = att.place("e_sum", [P, 1])
    r_sum = att.place("r_sum", [P, 1])
    score = att.place("score", [P, E])
    top_v = att.place("top_v", [P, 8])
    top_i = att.place("top_i", [P, 8], U32)
    top_if = att.place("top_if", [P, TOP_K])
    chosen = [att.place(f"chosen{i}", [P, TOP_K, E], BF16) for i in range(2)]
    any_choice = [att.place(f"any_choice{i}", [P, E], BF16) for i in range(2)]
    placed = att.place("placed", [P, TOP_K, E])
    place = att.place("place", [P, TOP_K])
    kept_from = att.at
    x1_sb = [att.place(f"x1_{i}", [P, D]) for i in range(NJ)]
    x1t_sb = [att.place(f"x1t{i}", [P, KC, P]) for i in range(2)]
    slot_of = att.place("slot_of", [P, NT, TOP_K], U32)
    pairs = att.place("pairs", [P, NT, TOP_K, 2], U32)

    chunk = 3 * KC * P * 4
    half = KC * BT * 4
    hi_at, lo_at = both.at, both.at + KC * chunk
    xs_at = lo_at + KC * chunk
    x_at = xs_at + 2 * BT * 4
    over_lo = Map(nc, lo_at, xs_at)
    su_hi = over_lo.place("su_hi", [P, KC, SI], F32R)
    su_lo = over_lo.place("su_lo", [P, KC, SI], F32R)
    sg_lo = over_lo.place("sg_lo", [P, KC, SI], F32R)
    hid_lo = over_lo.place("hid_lo", [P, SC, BT], F32R)
    over_hi = Map(nc, hi_at, lo_at)
    x1t_lo = over_hi.place("x1t_lo", [P, KC, BT], F32R)
    sg_hi = over_hi.place("sg_hi", [P, KC, SI], F32R)
    hid_hi = over_hi.place("hid_hi", [P, SC, BT], F32R)
    silu_s = over_hi.place("silu_s", [P, BT])
    hid_s = over_hi.place("hid_s", [P, BT])
    tanh_s = Map(nc, xs_at, x_at).place("tanh_s", [P, BT])
    x1t_stage = Map(nc, x_at, x_at + half).place("x1t_stage", [P, KC, BT])
    x1t_hi = Map(nc, x_at + 2 * half, x_at + 3 * half).place("x1t_hi", [P, KC, BT], F32R)
    sd_hi = Map(nc, x_at + half, x_at + 2 * half).place("sd_hi", [P, SC, D], F32R)
    sd_lo = Map(nc, x_at + 3 * half, x_at + 4 * half).place("sd_lo", [P, SC, D], F32R)
    shared_stage = Map(nc, both.at - 2 * 4 * (KC * GU + 2 * D), both.at)
    sg_stage = shared_stage.place("sg_stage", [P, KC, SI])
    su_stage = shared_stage.place("su_stage", [P, KC, SI])
    sd_stage = shared_stage.place("sd_stage", [P, SC, D])
    late = Map(nc, projected_end, kept_from)
    shared_rows = [late.place(f"shared_rows{b}", [P, NJ, D]) for b in range(NB - TAIL)]
    late_weights_at = late.at
    wgu_buf += [late.place(f"wgu{i}", [P, KC, GU]) for i in range(2, NG)]
    wdn_buf += [late.place(f"wdn{i}", [IH, 2, D]) for i in range(2, ND)]
    xg = [late.place(f"xg{i}", [P, D]) for i in range(3)]
    xgt_hi = [late.place(f"xgt_hi{i}", [P, KC, P], F32R) for i in range(2)]
    xgt_lo = [late.place(f"xgt_lo{i}", [P, KC, P], F32R) for i in range(2)]
    eo = [late.place(f"eo{i}", [P, D]) for i in range(2)]
    eo.append(Map(nc, x_at + 2 * half - 4 * D, x_at + 2 * half).place("eo2", [P, D]))
    tanh_e = late.place("tanh_e", [P, I])
    silu_e = late.place("silu_e", [P, I])
    hid_e = [late.place(f"hid_e{i}", [P, I]) for i in range(2)]
    hid_et = [late.place(f"hid_et{i}", [IH, 2, P]) for i in range(2)]
    assert late.at <= kept_from
    late.end, split_at = end, late.at
    wgu_hi = [late.place(f"wgu_hi{i}", [P, KC, GU], F32R) for i in range(2)]
    wgu_lo = [late.place(f"wgu_lo{i}", [P, KC, GU], F32R) for i in range(2)]
    fin_map = Map(nc, both.at - 2 * 4 * (KC * GU + 2 * D), both.at)
    fin_sb = [fin_map.place(f"fin{i}", [P, NJ, D]) for i in range(2)]
    fin_map = Map(nc, late_weights_at, late_weights_at + 4 * ((NG - 2) * KC * GU + (ND - 2) * 2 * D))
    fin_sb.append(fin_map.place("fin2", [P, NJ, D]))
    fin_map = Map(nc, split_at, late.at)
    fin_sb += [fin_map.place(f"fin{i}", [P, NJ, D]) for i in range(3, 6)]
    FINS = len(fin_sb)

    ctx = ExitStack()
    with ctx:
        def sem(name):
            return ctx.enter_context(nc.semaphore(name))

        banks = [ctx.enter_context(nc.psum_tensor(f"bank{i}", [P, 512], F32)) for i in range(8)]

        PE = Queue("PE", sem("pe"))
        DVE = Queue("DVE", sem("dve"))
        SCA = Queue("ACT", sem("act"))
        POOL = Queue("POOL", sem("pool"))
        SP = Queue("SP", None)
        V, S, G, M, Y = nc.vector, nc.scalar, nc.gpsimd, nc.tensor, nc.sync
        last = {}

        def lanes(name, n):
            return [Lane(sem(f"{name}{i}")) for i in range(n)]

        def load(name, dst, src, *ticks):
            return SP.dma(lambda: Y.dma_start(dst, src), Lane(sem(f"ld_{name}")), *ticks)

        def split(hi, lo, src, t_src, *left, pool=False):
            t_hi = SCA.do(lambda: S.copy(hi, src), t_src, *left)
            queue, engine = (POOL, G) if pool else (DVE, V)
            t_lo = queue.do(lambda: engine.tensor_tensor(lo, src, hi.bitcast(F32), ALU.subtract), t_hi, t_src, *left)
            return t_hi, t_lo

        def group(out_ap, products, *ticks, first=True, final=True):
            PE.wait(*ticks)
            n = len(products)
            for i, (a, b) in enumerate(products):
                start, stop = first and i == 0, final and i == n - 1
                make = lambda a=a, b=b, start=start, stop=stop: M.matmul(out_ap, a, b, start=start, stop=stop)
                t = PE.do(make) if stop else PE.quiet(make)
            return t

        def three(a_hi, a_lo, b_hi, b_lo):
            return [(a_hi, b_hi), (a_hi, b_lo), (a_lo, b_hi)]

        t = POOL.do(lambda: G.memset(ident[:, :], 0.0))
        t_ident = POOL.do(lambda: G.affine_select(
            out=ident[:, :], in_=ident[:, :], compare_op=ALU.not_equal, fill=1.0, base=0,
            pattern=[[-1, P]], channel_multiplier=1), t)
        t_ones = POOL.do(lambda: G.memset(ones[:, :], 1.0))
        t_before = POOL.do(lambda: G.affine_select(
            out=before[:, :], in_=ones[:, :], compare_op=ALU.is_ge, fill=0.0, base=-1,
            pattern=[[1, P]], channel_multiplier=-1), t_ones)
        t_before = POOL.do(lambda: G.affine_select(
            out=not_before[:, :], in_=ones[:, :], compare_op=ALU.is_ge, fill=0.0, base=0,
            pattern=[[-1, P]], channel_multiplier=1), t_ones)

        per_chunk = P // HW

        def head_mask(buf, rows_are_channels):
            t = POOL.do(lambda: G.memset(buf, 1.0))
            for sign, base in ((1, 0), (-1, HW - 1)):
                if rows_are_channels:
                    pattern, mult = [[sign * HW * per_chunk, KC], [-sign * HW, HEADS]], sign
                else:
                    pattern, mult = [[sign * HW * per_chunk, KC], [sign, P]], -sign * HW
                t = POOL.do(lambda pattern=pattern, mult=mult, base=base: G.affine_select(
                    out=buf, in_=buf, compare_op=ALU.is_ge, fill=0.0, base=base,
                    pattern=pattern, channel_multiplier=mult), t)
            return t

        t_sum = head_mask(head_sum[:, :, :], True)
        mask_f = kv[0:HEADS, :].rearrange("p (k c) -> p k c", k=KC)
        t = head_mask(mask_f, False)
        t_send = POOL.do(lambda: G.tensor_copy(head_send[:, :, :], mask_f), t)
        last["kv"] = (t_send,)
        t_expert_no = POOL.do(lambda: G.iota(expert_no[:, :], pattern=[[1, E]], base=0, channel_multiplier=0,
                                             allow_small_or_imprecise_dtypes=True))
        t_half = POOL.do(lambda: G.memset(minus_half[:, :], -0.5))
        t_token = POOL.do(lambda: G.iota(pairs[:, :, :, 0], pattern=[[P, NT], [0, TOP_K]], base=0,
                                         channel_multiplier=1))
        t1 = POOL.do(lambda: G.iota(table_sb[:, :, 0], pattern=[[0, E]], base=T, channel_multiplier=0))
        t2 = POOL.do(lambda: G.iota(table_sb[:, :, 1], pattern=[[0, E]], base=0, channel_multiplier=0))
        table_v = table_dram.rearrange("(s e) w -> s e w", e=E)

        num_ring, x1_ring = Ring(num), Ring(x1_sb)
        stage_lane = lanes("stage_lane", len(x1_sb))
        wq_v = w_qkv.rearrange("(k p) n -> p k n", p=P)
        wqkv_ready, wout_ready = {}, {}

        stage_plan, stage_loaded = [], []

        def stage_load():
            if stage_plan:
                src, hi, lo, ready, key = stage_plan.pop(0)
                slot, buf, left = x1_ring.take()
                view = buf[:, :] if len(hi.shape) == 2 else buf[:, :].rearrange("p (k n) -> p k n", k=KC)
                t = SP.dma(lambda: Y.dma_start(view, src), stage_lane[slot], *left)
                stage_loaded.append((slot, view, t, hi, lo, ready, key))

        def stage_split():
            slot, view, t, hi, lo, ready, key = stage_loaded.pop(0)
            ready[key] = split(hi, lo, view, t)
            x1_ring.leave(slot, *ready[key])
            stage_load()

        x_ring, x_lane = Ring(x_stage), lanes("x_lane", 2)
        x_staged, x_ready, x_left = {}, {}, {}

        def load_x(b, k):
            slot, buf, left = x_ring.take()
            src = x_t[k * P:(k + 1) * P, b * BT:(b + 1) * BT]
            x_staged[b, k] = slot, buf, SP.dma(lambda: Y.dma_start(buf[:, :], src), x_lane[slot], *left)

        def split_x(b, k):
            i = b % 2
            slot, buf, t = x_staged[b, k]
            x_ready[b, k] = split(x_hi[i][:, k, :], x_lo[i][:, k, :], buf[:, :], t, x_left.get(b - 2), pool=b > 0)
            x_ring.leave(slot, *x_ready[b, k])

        decay_in = load("decay", decay[:, :], decay_param)
        PARTS = (1, 2, 0)

        def plan_qkv(c, n):
            cols = slice(PARTS[n] * D + c * P, PARTS[n] * D + (c + 1) * P)
            i = 3 * c + n
            stage_plan.append((wq_v[:, :, cols], wqkv_hi[:, i, :, :], wqkv_lo[:, i, :, :], wqkv_ready, (c, n)))

        plan_qkv(0, 0)
        for k in (2, 3):
            stage_plan.append((x_t[k * P:(k + 1) * P, 0:BT], x_hi[0][:, k, :], x_lo[0][:, k, :], x_ready, (0, k)))
        for c in range(KC):
            for n in range(3):
                plan_qkv(c, n) if c + n else None
        for k in range(KC):
            stage_plan.append((w_out[k * P:(k + 1) * P, :], wout_hi[:, k, :], wout_lo[:, k, :], wout_ready, k))

        load_x(0, 0)
        load_x(0, 1)
        for _ in x1_sb:
            stage_load()
        split_x(0, 0)
        split_x(0, 1)
        for _ in range(3 + 2):
            stage_split()
        load_x(1, 0)
        load_x(1, 1)
        gate_in = load("gate", gate_sb[:, :, :], gate_t.rearrange("(k p) n -> p k n", p=P))
        table_empty = load("table_empty", table_v, table_sb[:, :, :], t1, t2)
        t = SCA.do(lambda: S.activation(decay[:, :], decay[:, :], ACT.Exp, scale=-1.0), decay_in)
        t = DVE.do(lambda: V.tensor_scalar(decay[:, :], decay[:, :], 1.0, None, ALU.add), t)
        t_decay = DVE.do(lambda: V.reciprocal(decay[:, :], decay[:, :]), t)
        t_state = DVE.do(lambda: V.memset(state[:, :, :], 0.0))

        ps_proj = Ring(banks[0:3])
        e_ring, relu_ring, qk_ring = Ring(e_sb), Ring(relu_sb), Ring(qk)
        num_ready, qk_ready, state_tick = {}, {}, {}

        def project_group(b, c, n):
            slot, ps, left = ps_proj.take()
            xh, xl = x_hi[b % 2], x_lo[b % 2]
            i = 3 * c + n
            PE.wait(*wqkv_ready[c, n], *left)
            for k in range(KC):
                PE.wait(*x_ready[b, k])
                mm = group(ps[:, :], three(wqkv_hi[:, i, k, :], wqkv_lo[:, i, k, :], xh[:, k, :], xl[:, k, :]),
                           first=(k == 0), final=(k == KC - 1))
            return slot, ps, mm

        def feature_map(dst, n, b, c, *dst_left):
            slot, ps, mm = project_group(b, c, n)
            es, e, e_left = e_ring.take()
            rs, r, r_left = relu_ring.take()
            te = SCA.do(lambda: S.activation(e[:, :], ps[:, :], ACT.Exp), mm, *e_left)
            tr = SCA.do(lambda: S.activation(r[:, :], ps[:, :], ACT.Relu), *r_left)
            ps_proj.leave(slot, tr)
            t = DVE.do(lambda: V.scalar_tensor_tensor(out=dst[:, :], in0=e[:, :], scalar=1.0, in1=r[:, :],
                                                      op0=ALU.min, op1=ALU.add), te, tr, *dst_left)
            e_ring.leave(es, t)
            relu_ring.leave(rs, t)
            return t, mm

        projected = {}
        running = {}

        def project_k(b, c):
            running["k"], _ = feature_map(phi_k, 0, b, c, *last.get("phi_k", ()))

        def scan_k(b, c):
            dec = decay[:, c:c + 1].to_broadcast([P, BT])
            running["rk"] = DVE.do(lambda: V.tensor_tensor_scan(
                out=run_k[:, :], data0=dec, data1=phi_k[:, :], initial=state[:, c, 0:1],
                op0=ALU.mult, op1=ALU.add), running["k"], t_decay, t_state, state_tick.get(c), *last.get("run_k", ()))

        def project_v(b, c):
            running["v"] = project_group(b, c, 1)

        def scan_kv(b, c):
            slot, ps, mm_v = running["v"]
            dec = decay[:, c:c + 1].to_broadcast([P, BT])
            t_kv = DVE.do(lambda: V.tensor_tensor(kv[:, :], phi_k[:, :], ps[:, :], ALU.mult),
                          mm_v, *last.get("kv", ()))
            ps_proj.leave(slot, t_kv)
            last["phi_k"] = (running["rk"], t_kv)
            running["rkv"] = DVE.do(lambda: V.tensor_tensor_scan(
                out=run_kv[:, :], data0=dec, data1=kv[:, :], initial=state[:, c, 1:2],
                op0=ALU.mult, op1=ALU.add), t_kv, *last.get("run_kv", ()))
            last["kv"] = (running["rkv"],)

        def project_q(b, c):
            t_q, mm_q = feature_map(phi_q, 2, b, c, *last.get("phi_q", ()))
            projected[b, c] = mm_q
            if c == KC - 1:
                x_left[b] = mm_q
            t_sk = SCA.do(lambda: S.copy(state[:, c, 0:1], run_k[:, BT - 1:BT]), running["rk"])
            t_skv = SCA.do(lambda: S.copy(state[:, c, 1:2], run_kv[:, BT - 1:BT]), running["rkv"])
            state_tick[c] = t_skv
            qs, qkb, q_left = qk_ring.take()
            t_qk = DVE.do(lambda: V.tensor_tensor(qkb[:, :], phi_q[:, :], run_k[:, :], ALU.mult), t_q, *q_left)
            ns, nm, n_left = num_ring.take()
            t_num = POOL.do(lambda: G.tensor_tensor(nm[:, :], phi_q[:, :], run_kv[:, :], ALU.mult),
                            t_q, running["rkv"], *n_left)
            last["run_k"] = (t_qk, t_sk)
            last["run_kv"] = (t_num, t_skv)
            last["phi_q"] = (t_qk, t_num)
            qk_ready[b, c] = (qs, qkb, t_qk)
            num_ready[b, c] = (ns, nm, t_num)

        ps_send, ps_small = Ring(banks[6:7]), Ring(banks[5:6])
        den_tick, att_ready, att_left, att_open = {}, {}, {}, []

        def sum_heads(b, tiles):
            slot, ps, left = ps_small.take()
            for j in tiles:
                mm = group(ps[:, j * HEADS:(j + 1) * HEADS],
                           [(qk_ready[b, c][1][:, j * P:(j + 1) * P], head_sum[:, c, :]) for c in range(KC)],
                           *[qk_ready[b, c][2] for c in range(KC)], t_sum, *left)
            if j == NJ - 1:
                for c in range(KC):
                    qk_ring.leave(qk_ready[b, c][0], mm)
            cols = slice(tiles[0] * HEADS, (j + 1) * HEADS)
            flat = rden[:, :, :].rearrange("p j h -> p (j h)")[:, cols]
            t = DVE.do(lambda: V.tensor_scalar(flat, ps[:, cols], EPS_DEN, None, ALU.max),
                       mm, *last.get("rden", ()))
            ps_small.leave(slot, t)
            den_tick[b] = DVE.do(lambda: V.reciprocal(flat, flat), t)

        def turn_rden(b):
            slot, ps, left = ps_send.take()
            PE.wait(den_tick[b], t_ident, *left)
            for j in range(NJ):
                make = lambda j=j: M.transpose(ps[0:HEADS, j * P:(j + 1) * P], rden[:, j, :], ident[:, :])
                mm = PE.do(make) if j == NJ - 1 else PE.quiet(make)
            last["rden"] = (mm,)
            den_tick[b] = split(rden_hi[:, :], rden_lo[:, :], ps[0:HEADS, :], mm, *last.get("rden_hi", ()))
            ps_send.leave(slot, *den_tick[b])

        def divide(b, c):
            slot, ps, left = ps_send.take()
            mm = group(ps[:, :], [(head_send[:, c, :], rden_hi[:, :]), (head_send[:, c, :], rden_lo[:, :])],
                       t_send, *den_tick[b], *left)
            ns, nm, t_num = num_ready[b, c]
            t = DVE.do(lambda: V.tensor_tensor(nm[:, :], nm[:, :], ps[:, :], ALU.mult), mm, t_num)
            ps_send.leave(slot, t)
            last["rden_hi"] = (mm,)
            att_open.append((b, c, ns, nm, t))

        def split_att():
            b, c, ns, nm, t = att_open.pop(0)
            att_ready[b, c] = split(att_hi[:, c, :], att_lo[:, c, :], nm[:, :], t, att_left.get(b - 1))
            num_ring.leave(ns, *att_ready[b, c])

        xres_ring, xres_lane, xres_ready = Ring(xres), lanes("xres_lane", len(xres)), {}

        def load_xres(b, j):
            slot, buf, left = xres_ring.take()
            row = b * BT + j * P
            t = SP.dma(lambda: Y.dma_start(buf[:, :], x[row:row + P, :]), xres_lane[slot], *left)
            xres_ready[b, j] = (slot, buf, t)

        norms = [0]

        def norm(buf, t_src):
            i = norms[0] % len(mv)
            norms[0] += 1
            t = DVE.do(lambda: V.bn_stats(stats[:, :], buf), t_src, *last.get("stats", ()))
            t_mv = DVE.do(lambda: V.bn_aggr(mv[i][:, :], stats[:, :]), t, *last.get(f"mv{i}", ()))
            last["stats"] = (t_mv,)
            t = POOL.do(lambda: G.tensor_scalar(rstd[i][:, :], mv[i][:, 1:2], EPS_NORM, None, ALU.add),
                        t_mv, *last.get(f"mv{i}", ()))
            t_r = POOL.do(lambda: G.tensor_tensor(rstd[i][:, :], rstd[i][:, :], minus_half[:, :], ALU.pow), t, t_half)

            t_b = POOL.do(lambda: G.tensor_scalar(shift[i][:, :], mv[i][:, 0:1], rstd[i][:, 0:1], -1.0,
                                                  ALU.mult, ALU.mult), t_r)

            def apply():
                t = SCA.do(lambda: S.activation(buf, buf, ACT.Identity, bias=shift[i][:, 0:1],
                                                scale=rstd[i][:, 0:1]), t_b, t_mv)
                last[f"mv{i}"] = (t,)
                return t
            return apply

        ps_rows_a = Ring(banks[4:5])
        x1_lane = lanes("x1_lane", len(x1_sb))
        acc_lane = lanes("acc_lane", len(x1_sb))
        x1_ready, x1_stored, x1_open = {}, [], []

        def out_project(b, j):
            slot, ps, left = ps_rows_a.take()
            tok = slice(j * P, (j + 1) * P)
            products = []
            for k in range(KC):
                products += three(att_hi[:, k, tok], att_lo[:, k, tok], wout_hi[:, k, :], wout_lo[:, k, :])
            ready = [t for c in range(KC) for t in (*att_ready[b, c], *wout_ready[c])]
            mm = group(ps[:, :], products, *ready, *left)
            if j == NJ - 1:
                att_left[b] = mm
            xs, xr, t_x = xres_ready[b, j]
            x1s, x1, x1_left = x1_ring.take()
            t = DVE.do(lambda: V.tensor_tensor(x1[:, :], ps[:, :], xr[:, :], ALU.add), mm, t_x, *x1_left)
            ps_rows_a.leave(slot, t)
            xres_ring.leave(xs, t)
            if j + 2 < NJ:
                load_xres(b, j + 2)
            x1_open.append((b, j, x1s, x1, norm(x1[:, :], t)))

        def store_x1():
            b, j, x1s, x1, apply = x1_open.pop(0)
            t = apply()
            row = b * BT + j * P
            w1 = SP.dma(lambda: Y.dma_start(x1_dram[row:row + P, :], x1[:, :]), x1_lane[x1s], t)
            w2 = SP.dma(lambda: Y.dma_start(acc_dram[row:row + P, :], x1[:, :]), acc_lane[x1s], t)
            x1_stored.extend((w1, w2))
            x1_ready[b, j] = (x1s, x1, t, w1, w2)

        ps_turn, ps_count = Ring(banks[3:4]), banks[7]
        x1t_ring, x1t_lane, x1t_stored = Ring(x1t_sb), lanes("x1t_lane", len(x1t_sb)), {}
        chosen_ring = Ring(list(zip(chosen, any_choice)))
        scatter_lane = Lane(sem("scatter_lane"))
        scattered = []

        turned, routing = {}, {}

        def turn(b, j):
            slot, ps, left = ps_turn.take()
            x1s, x1, t_x1, w1, w2 = x1_ready[b, j]
            PE.wait(t_x1, t_ident, *left)
            for k in range(KC):
                make = lambda k=k: M.transpose(ps[:, k * P:(k + 1) * P], x1[:, k * P:(k + 1) * P], ident[:, :])
                mm = PE.do(make) if k == KC - 1 else PE.quiet(make)
            x1_ring.leave(x1s, mm, w1, w2)
            ts, x1t, t_left = x1t_ring.take()
            t = SCA.do(lambda: S.copy(x1t[:, :, :], ps[:, :].rearrange("p (k t) -> p k t", k=KC)), mm, *t_left)
            ps_turn.leave(slot, t)
            col = b * BT + j * P
            dst = x1t_dram.rearrange("(k p) t -> p k t", p=P)[:, :, col:col + P]
            w = SP.dma(lambda: Y.dma_start(dst, x1t[:, :, :]), x1t_lane[ts], t)
            x1t_stored[b, j] = w
            turned[b, j] = (ts, x1t, t, w)

        def score_experts(b, j):
            ts, x1t, t, w = turned[b, j]
            slot, logits, left = ps_small.take()
            mm = group(logits[:, 0:E], [(x1t[:, k, :], gate_sb[:, k, :]) for k in range(KC)], t, gate_in, *left)
            x1t_ring.leave(ts, mm, w)
            t = DVE.do(lambda: V.tensor_reduce(neg_max[:, :], logits[:, 0:E], AX.X, ALU.max, negate=True),
                       mm, *last.get("neg_max", ()))
            t_e = SCA.do(lambda: S.activation(e_route[:, :], logits[:, 0:E], ACT.Exp, bias=neg_max[:, 0:1],
                                              accum_out=e_sum[:, :]), t, *last.get("e_route", ()))
            last["neg_max"] = (t_e,)
            ps_small.leave(slot, t_e)
            routing[b, j] = t_e

        def choose(b, j):
            i = b * NJ + j
            t_e = routing[b, j]
            t = DVE.do(lambda: V.reciprocal(r_sum[:, :], e_sum[:, :]), t_e, *last.get("r_sum", ()))
            t_s = DVE.do(lambda: V.tensor_scalar(score[:, :], e_route[:, :], r_sum[:, 0:1], None, ALU.mult),
                         t, *last.get("score", ()))
            last["e_route"] = last["r_sum"] = (t_s,)
            t_v = DVE.do(lambda: V.max(top_v[:, :], score[:, :]), t_s, *last.get("top_v", ()))
            t_i = DVE.do(lambda: V.max_index(top_i[:, :], top_v[:, :], score[:, :]), t_v, *last.get("top_i", ()))
            last["score"] = (t_i,)
            t_w = SCA.do(lambda: S.copy(pairs[:, i, :, 1].bitcast(F32), top_v[:, 0:TOP_K]), t_v, t_token)
            last["top_v"] = (t_w, t_i)
            t_f = DVE.do(lambda: V.tensor_copy(top_if[:, :], top_i[:, 0:TOP_K]), t_i, *last.get("top_if", ()))
            last["top_i"] = (t_f,)
            cs, (ch, any_ch), c_left = chosen_ring.take()
            t_c = DVE.do(lambda: V.tensor_tensor(
                ch[:, :, :], expert_no[:, :].unsqueeze(1).to_broadcast([P, TOP_K, E]),
                top_if[:, :].unsqueeze(2).to_broadcast([P, TOP_K, E]), ALU.is_equal),
                t_f, t_expert_no, *c_left)
            t_any = DVE.do(lambda: V.tensor_reduce(any_ch[:, :], ch[:, :, :].rearrange("p k e -> p e k"), AX.X, ALU.max),
                           t_c)
            routing[b, j] = (cs, ch, any_ch, t_any, t_w)

        def count_before(b, j):
            i = b * NJ + j
            cs, ch, any_ch, t_any, t_w = routing[b, j]
            mm = PE.do(lambda: M.matmul(ps_count[:, 0:E], before[:, :], any_ch[:, :], start=(i == 0), stop=True,
                                        skip_group_check=(i > 0)), t_any, t_before, *last.get("ps_count", ()))
            routing[b, j] = (cs, ch, any_ch, mm, t_w)

        def place_choices(b, j):
            i = b * NJ + j
            cs, ch, any_ch, mm, t_w = routing[b, j]
            t_p = DVE.do(lambda: V.tensor_tensor(
                placed[:, :, :], ch[:, :, :], ps_count[:, 0:E].unsqueeze(1).to_broadcast([P, TOP_K, E]), ALU.mult),
                mm, *last.get("placed", ()))
            last["ps_count"] = (t_p,)
            t_pl = DVE.do(lambda: V.tensor_reduce(place[:, :], placed[:, :, :], AX.X, ALU.add), t_p, *last.get("place", ()))
            last["placed"] = (t_pl,)
            t_slot = DVE.do(lambda: V.scalar_tensor_tensor(
                out=slot_of[:, i, :], in0=place[:, :], scalar=float(E), in1=top_if[:, :], op0=ALU.mult, op1=ALU.add), t_pl)
            last["place"] = last["top_if"] = (t_slot,)
            routing[b, j] = (cs, any_ch, t_p, t_slot, t_w)

        def count_rest(b, j):
            cs, any_ch, t_p, t_slot, t_w = routing[b, j]
            mm = PE.do(lambda: M.matmul(ps_count[:, 0:E], not_before[:, :], any_ch[:, :], start=False, stop=True,
                                        skip_group_check=True), t_p)
            chosen_ring.leave(cs, t_p, mm)

        def scatter_choices(b, j):
            i = b * NJ + j
            cs, any_ch, t_p, t_slot, t_w = routing[b, j]
            for k in range(TOP_K):
                scattered.append(POOL.dma(lambda k=k: G.indirect_dma_start(
                    table_dram, bass.IndirectOffsetOnAxis(slot_of[:, i, k:k + 1], 0), pairs[:, i, k, :], None,
                    bounds_check=SLOTS - 1, oob_is_err=False), scatter_lane, t_slot, t_w, table_empty))

        gu_lane, dn_lane = lanes("gu_lane", NG), lanes("dn_lane", ND)
        gu_ready, dn_ready, w_left, w_split = {}, {}, {}, {}

        def load_gate_up(e):
            s = e % NG
            gu_ready[e] = SP.dma(lambda: Y.dma_start(wgu_buf[s][:, :, :], w_gu[e].rearrange("(k p) n -> p k n", p=P)),
                                 gu_lane[s], *w_split.get(e - NG, ()))

        def load_down(e):
            s = e % ND
            dn_ready[e] = SP.dma(lambda: Y.dma_start(wdn_buf[s][:, :, :], w_down[e].rearrange("(h p) n -> p h n", p=IH)),
                                 dn_lane[s], w_left.get(e - ND))

        shared_lane = lanes("shared_lane", 1)[0]
        shared_w = {}

        def load_shared(name, view, src):
            shared_w[name] = view, load("shared_" + name, view[:, :, :], src)

        def split_shared(name, hi, lo, t_free):
            view, t = shared_w[name]
            shared_w[name] = split(hi[:, :, :], lo[:, :, :], view[:, :, :], t, t_free, pool=True)

        x1t_split, hid_ready, rows_ready = {}, {}, {}

        def shared_load(b):
            src = x1t_dram.rearrange("(k p) t -> p k t", p=P)[:, :, b * BT:(b + 1) * BT]
            t = SP.dma(lambda: Y.dma_start(x1t_stage[:, :, :], src), shared_lane,
                       x_left[NB - 2], *[x1t_stored[b, j] for j in range(NJ)], *last.get("x1t_stage", ()))
            x1t_split[b] = t

        def shared_split(b):
            ticks = []
            SCA.wait(x_left[NB - 2])
            DVE.wait(projected[NB - 1, 1])
            for k in range(KC):
                ticks += split(x1t_hi[:, k, :], x1t_lo[:, k, :], x1t_stage[:, k, :], x1t_split[b], *last.get("x1t_hi", ()))
            last["x1t_stage"] = x1t_split[b] = tuple(ticks)

        def shared_up(b, c):
            cols = slice(c * P, (c + 1) * P)
            gs, psg, g_left = ps_proj.take()
            products = []
            for k in range(KC):
                products += three(sg_hi[:, k, cols], sg_lo[:, k, cols], x1t_hi[:, k, :], x1t_lo[:, k, :])
            mm_g = group(psg[:, :], products, *shared_w["g"], *x1t_split[b], *g_left)
            t = SCA.do(lambda: S.activation(tanh_s[:, :], psg[:, :], ACT.Tanh, scale=0.5), mm_g, *last.get("tanh_s", ()))
            t_silu = DVE.do(lambda: V.scalar_tensor_tensor(out=silu_s[:, :], in0=tanh_s[:, :], scalar=1.0, in1=psg[:, :],
                                                           op0=ALU.add, op1=ALU.mult), t, *last.get("silu_s", ()))
            last["tanh_s"] = (t_silu,)
            ps_proj.leave(gs, t_silu)
            yield
            us, psu, u_left = ps_proj.take()
            products = []
            for k in range(KC):
                products += three(su_hi[:, k, cols], su_lo[:, k, cols], x1t_hi[:, k, :], x1t_lo[:, k, :])
            mm_u = group(psu[:, :], products, *shared_w["u"], *u_left)
            if c == SC - 1:
                last["x1t_hi"] = (mm_u,)
            t = DVE.do(lambda: V.scalar_tensor_tensor(out=hid_s[:, :], in0=silu_s[:, :], scalar=0.5, in1=psu[:, :],
                                                      op0=ALU.mult, op1=ALU.mult), t_silu, mm_u, *last.get("hid_s", ()))
            last["silu_s"] = (t,)
            ps_proj.leave(us, t)
            hid_ready[b, c] = split(hid_hi[:, c, :], hid_lo[:, c, :], hid_s[:, :], t, *last.get("hid_hi", ()))
            last["hid_s"] = hid_ready[b, c]
            yield

        def shared_down(b, pair):
            slots = [ps_proj.take() for _ in pair]
            for late_chunk in (False, True):
                for j, (slot, ps, left) in zip(pair, slots):
                    tok = slice(j * P, (j + 1) * P)
                    chunks = [SC - 1] if late_chunk else range(SC - 1)
                    PE.wait(*shared_w["d"], *left, *[t for c in chunks for t in hid_ready[b, c]])
                    for c in chunks:
                        mm = group(ps[:, :], three(hid_hi[:, c, tok], hid_lo[:, c, tok], sd_hi[:, c, :], sd_lo[:, c, :]),
                                   first=(c == 0), final=late_chunk)
                    if late_chunk:
                        rows_ready[b, j] = mm
            if pair[-1] == NJ - 1:
                last["hid_hi"] = (mm,)
            for j, (slot, ps, left) in zip(pair, slots):
                mm = rows_ready[b, j]
                if b < NB - TAIL:
                    t = SCA.do(lambda b=b, j=j, ps=ps: S.copy(shared_rows[b][:, j, :], ps[:, :]), mm, *rows_free)
                    ps_proj.leave(slot, t)
                    rows_ready[b, j] = (shared_rows[b][:, j, :], t, None)
                else:
                    rows_ready[b, j] = (ps[:, :], mm, slot)

        def shared_units():
            for b in range(NB):
                if b + 1 < NB:
                    shared_load(b + 1)
                for c in range(SC):
                    yield from shared_up(b, c)
                if b + 1 < NB:
                    shared_split(b + 1)
                for pair in ((0, 1), (2, 3)):
                    shared_down(b, pair)
                    for j in pair if b >= NB - TAIL else ():
                        finish_tile(b, j)
                    yield
        UNITS = 2 * SC + NJ // 2
        units = shared_units()
        done_units = [0]

        def fill():
            next(units)
            done_units[0] += 1

        OUT = {(3, 0): (1, 0), (3, 2): (1, 1), (0, 0): (2, 2), (0, 2): (2, 3)}
        DIVIDE = {(1, 0): 0, (1, 1): 1, (1, 2): 2, (2, 1): 3}

        def mix_piece(it, c, at):
            if (c, at) in DIVIDE and 0 <= it - 1 < NB:
                divide(it - 1, DIVIDE[c, at])
            if (c, at) in OUT:
                back, j = OUT[c, at]
                if 0 <= it - back < NB:
                    out_project(it - back, j)
            if c == 0 and 0 <= it - 1 < NB:
                if at < 2:
                    sum_heads(it - 1, range(at * NJ // 2, (at + 1) * NJ // 2))

        def stage_next(it, c, n):
            if it == 0:
                for _ in range(1 if c + 1 < KC or n < 2 else 2):
                    stage_split()

        def attention_step(it, c):
            working = it < NB
            n = it * KC + c - 2 * KC
            tile = (n // KC, n % KC) if 0 <= n < NT else None
            n -= 1
            before_tile = (n // KC, n % KC) if 0 <= n < NT else None
            if before_tile:
                choose(*before_tile)
            if it + 1 < NB:
                split_x(it + 1, c)
                ahead = (it + 1) * KC + c + 2
                if ahead < NB * KC:
                    load_x(ahead // KC, ahead % KC)
            if working:
                project_k(it, c)
                stage_next(it, c, 0)
            else:
                fill()
            while att_open:
                split_att()
            mix_piece(it, c, 0)
            if working:
                project_v(it, c)
                stage_next(it, c, 1)
            elif (it == NB and c > 0) or it == NB + 1:
                fill()
            if before_tile:
                count_before(*before_tile)
            if working:
                scan_k(it, c)
            if before_tile:
                place_choices(*before_tile)
            while att_open:
                split_att()
            if tile:
                turn(*tile)
            if working:
                scan_kv(it, c)
            while x1_open:
                store_x1()
            mix_piece(it, c, 1)
            if working:
                project_q(it, c)
                stage_next(it, c, 2)
            else:
                fill()
            while att_open:
                split_att()
            if c == 0 and 0 <= it - 1 < NB:
                turn_rden(it - 1)
            if before_tile:
                count_rest(*before_tile)
            if tile:
                score_experts(*tile)
            mix_piece(it, c, 2)
            if before_tile:
                scatter_choices(*before_tile)
            if c == 1 and 0 <= it - 1 < NB:
                load_xres(it - 1, 0)
                load_xres(it - 1, 1)

        fin_lane, fin_out = lanes("fin_lane", FINS), lanes("fin_out", NJ // 2 * FINS)
        fin_buf, added, written, written_of, open_norms, to_load = {}, [None], [], {}, [], []
        fin_ring = Ring(fin_sb)

        def finish_load(b):
            slot, buf, left = fin_ring.take()
            src = acc_dram[b * BT:(b + 1) * BT, :].rearrange("(j p) d -> p j d", p=P)
            t = SP.dma(lambda: Y.dma_start(buf[:, :, :], src), fin_lane[slot], added[0], w_left[E - 1], *left)
            fin_buf[b] = slot, buf, t

        def finish_tile(b, j):
            slot, buf, t_in = fin_buf[b]
            z = buf[:, j, :]
            rows, t_rows, rows_slot = rows_ready[b, j]
            t = DVE.do(lambda: V.tensor_tensor(z, rows, z, ALU.add), t_in, t_rows)
            if rows_slot is not None:
                ps_proj.leave(rows_slot, t)
            open_norms.append((b, j, norm(z, t)))
            if len(open_norms) > 2:
                finish_norm()

        def finish_norm():
            b, j, apply = open_norms.pop(0)
            slot, buf, t_in = fin_buf[b]
            t = apply()
            if j % 2:
                dst = out[b * BT + (j - 1) * P:b * BT + (j + 1) * P, :].rearrange("(j p) d -> p j d", p=P)
                w = SP.dma(lambda: Y.dma_start(dst, buf[:, j - 1:j + 1, :]), fin_out[NJ // 2 * slot + j // 2], t)
                written.append(w)
                written_of.setdefault(b, []).append(w)
                if j == NJ - 1:
                    fin_ring.leave(slot, *written_of.pop(b), w)
                    if to_load:
                        finish_load(to_load.pop(0))

        for it in range(NB):
            for c in range(KC):
                attention_step(it, c)
                if (it, c) == (1, 0):
                    load_shared("g", sg_stage, sg_t.rearrange("(k p) n -> p k n", p=P))
                    load_shared("u", su_stage, su_t.rearrange("(k p) n -> p k n", p=P))
                    load_shared("d", sd_stage, sd_t.rearrange("(k p) n -> p k n", p=P))
                if it == NB - 1:
                    if c == 0:
                        shared_load(0)
                    if c == 1:
                        split_shared("u", su_hi, su_lo, projected[it, 1])
                    if c == 2:
                        split_shared("g", sg_hi, sg_lo, projected[it, 2])
                        shared_split(0)
                    if c == 3:
                        split_shared("d", sd_hi, sd_lo, projected[it, 3])
        SP.wait(*[t for name in "gud" for t in shared_w[name]])
        for e in range(2):
            load_gate_up(e)
            load_down(e)
        rows_free = ()
        for it in (NB, NB + 1):
            for c in range(KC):
                attention_step(it, c)
                if (it, c) == (NB, 0):
                    rows_free = tuple((q.sem, q.count) for q in (PE, DVE, SCA, POOL))
        attention_step(NB + 2, 0)
        attention_end = tuple((q.sem, q.count) for q in (PE, DVE, SCA, POOL))
        rows_free = attention_end

        table_in = load("table_in", table_sb[:, :, :], table_v, scattered[-1], table_empty)
        ps_xg, ps_gu, ps_ht, ps_eo = Ring(banks[3:4]), Ring(banks[4:6]), Ring(banks[6:7]), Ring(banks[7:8])
        xg_ring, xgt_ring, eo_ring = Ring(xg), Ring(list(zip(xgt_hi, xgt_lo))), Ring(eo)
        hid_e_ring, hid_et_ring = Ring(hid_e), Ring(hid_et)
        xg_lane, add_lane = lanes("xg_lane", len(xg)), Lane(sem("add_lane"))
        xg_ready, xgt_ready, hid_e_ready, gated = {}, {}, {}, {}

        def gather(e):
            slot, buf, left = xg_ring.take()
            t = POOL.dma(lambda: G.indirect_dma_start(
                buf[:, :], None, x1_dram, bass.IndirectOffsetOnAxis(table_sb[:, e, 0:1], 0),
                bounds_check=T - 1, oob_is_err=False), xg_lane[slot], table_in, *left)
            xg_ready[e] = (slot, buf, t)

        def turn_rows(e):
            gs, buf, t_g = xg_ready[e]
            ps_slot, ps, left = ps_xg.take()
            PE.wait(t_g, *left)
            for k in range(KC):
                make = lambda k=k: M.transpose(ps[:, k * P:(k + 1) * P], buf[:, k * P:(k + 1) * P], ident[:, :])
                mm = PE.do(make) if k == KC - 1 else PE.quiet(make)
            xg_ring.leave(gs, mm)
            ts, (hi, lo), t_left = xgt_ring.take()
            t = split(hi[:, :, :], lo[:, :, :], ps[:, :].rearrange("p (k s) -> p k s", k=KC), mm, *t_left)
            ps_xg.leave(ps_slot, *t)
            xgt_ready[e] = (ts, hi, lo, t)

        def split_expert(e):
            s = e % 2
            w = wgu_buf[e % NG]
            t = split(wgu_hi[s][:, :, :], wgu_lo[s][:, :, :], w[:, :, :], gu_ready[e], table_in, *x1_stored,
                      *x1t_stored.values(), gated.get(e - 2))
            w_split[e] = t

        def gate_up(e):
            ts, x_hi_e, x_lo_e, t_x = xgt_ready[e]
            slot, ps, left = ps_gu.take()
            w_hi_e, w_lo_e = wgu_hi[e % 2], wgu_lo[e % 2]
            products = []
            for k in range(KC):
                products += three(x_hi_e[:, k, :], x_lo_e[:, k, :], w_hi_e[:, k, :], w_lo_e[:, k, :])
            gated[e] = mm = group(ps[:, 0:GU], products, *t_x, *w_split[e], *left)
            xgt_ring.leave(ts, mm)
            t = SCA.do(lambda: S.activation(tanh_e[:, :], ps[:, 0:I], ACT.Tanh, scale=0.5), mm, *last.get("tanh_e", ()))
            t = DVE.do(lambda: V.scalar_tensor_tensor(out=silu_e[:, :], in0=tanh_e[:, :], scalar=1.0, in1=ps[:, 0:I],
                                                      op0=ALU.add, op1=ALU.mult), t, *last.get("silu_e", ()))
            last["tanh_e"] = (t,)
            hs, h, h_left = hid_e_ring.take()
            t = DVE.do(lambda: V.scalar_tensor_tensor(out=h[:, :], in0=silu_e[:, :], scalar=0.5, in1=ps[:, I:GU],
                                                      op0=ALU.mult, op1=ALU.mult), t, *h_left)
            last["silu_e"] = (t,)
            ps_gu.leave(slot, t)
            hid_e_ready[e] = (hs, h, t)

        def turn_hidden(e):
            hs, h, t_h = hid_e_ready[e]
            slot, ps, left = ps_ht.take()
            PE.wait(t_h, *left)
            for k in range(2):
                make = lambda k=k: M.transpose(ps[0:IH, k * P:(k + 1) * P], h[:, k * IH:(k + 1) * IH], ident[:, :])
                mm = PE.do(make) if k else PE.quiet(make)
            hid_e_ring.leave(hs, mm)
            ts, ht, t_left = hid_et_ring.take()
            t = SCA.do(lambda: S.copy(ht[:, :, :], ps[0:IH, 0:2 * P].rearrange("p (h s) -> p h s", h=2)), mm, *t_left)
            ps_ht.leave(slot, t)
            return ts, ht, t

        def down(e, ts, ht, t):
            slot, ps, left = ps_eo.take()
            w = wdn_buf[e % ND]
            mm = group(ps[:, :], [(ht[:, k, :], w[:, k, :]) for k in range(2)], t, dn_ready[e], *left)
            hid_et_ring.leave(ts, mm)
            w_left[e] = mm
            es, eob, e_left = eo_ring.take()
            t = SCA.do(lambda: S.activation(eob[:, :], ps[:, :], ACT.Copy, scale=table_sb[:, e, 1:2].bitcast(F32)),
                       mm, table_in, *e_left)
            ps_eo.leave(slot, t)
            return es, eob, t

        def add_rows(e, es, eob, t):
            a = POOL.dma(lambda: G.indirect_dma_start(
                acc_dram, bass.IndirectOffsetOnAxis(table_sb[:, e, 0:1], 0), eob[:, :], None,
                bounds_check=T - 1, oob_is_err=False, compute_op=ALU.add), add_lane, t, added[0])
            added[0] = a
            eo_ring.leave(es, a)

        COVER = 6
        for q in (SP, DVE, SCA, POOL):
            q.wait(*attention_end)
        POOL.wait(*x1_stored)
        for e in range(2, NG):
            load_gate_up(e)
        for e in range(2, ND):
            load_down(e)
        AHEAD = len(xg)
        for e in range(AHEAD - 1):
            gather(e)
        for _ in range(COVER - 3):
            fill()
        for e in range(2):
            split_expert(e)
            load_gate_up(e + NG)
        for _ in range(2):
            fill()
        PE.wait(*attention_end)
        turn_rows(0)
        fill()
        pending = turned = None
        total, before_units = (NB - TAIL) * UNITS, done_units[0]
        for e in range(E):
            if e + AHEAD - 1 < E:
                gather(e + AHEAD - 1)
            gate_up(e)
            if e + 1 < E:
                turn_rows(e + 1)
            if e + 2 < E:
                split_expert(e + 2)
            if e + 2 + NG < E:
                load_gate_up(e + 2 + NG)
            if pending:
                add_rows(*pending)
            if turned:
                pending = (e - 1, *down(e - 1, *turned))
                if e - 1 + ND < E:
                    load_down(e - 1 + ND)
            while done_units[0] < total and (done_units[0] - before_units) * E < (e + 1) * (total - before_units):
                fill()
            turned = turn_hidden(e)
        add_rows(*pending)
        add_rows(E - 1, *down(E - 1, *turned))

        early = [(b, j) for b in range(NB - TAIL) for j in range(NJ)]
        SKIP, UNITS_LEFT = 7, TAIL * UNITS

        def early_done(i):
            return min(len(early), max(0, (i + 1 - SKIP) * len(early) // (UNITS_LEFT - 1 - SKIP)))

        order = []
        for i in range(UNITS_LEFT):
            if (i + 1) % UNITS == 0:
                order.append(NB - TAIL + i // UNITS)
            order += [early[n][0] for n in range(early_done(i - 1), early_done(i)) if early[n][1] == NJ - 1]
        for i in range(UNITS_LEFT):
            fill()
            if i == 0:
                for b in order[0:FINS]:
                    finish_load(b)
                to_load.extend(order[FINS:])
            for n in range(early_done(i - 1), early_done(i)):
                finish_tile(*early[n])
        while open_norms:
            finish_norm()
        SP.wait(*written)

        block = ctx.enter_context(nc.Block())

        @block.sync
        def _(eng):
            SP.flush(eng)

        @block.scalar
        def _(eng):
            SCA.flush(eng)

        @block.vector
        def _(eng):
            DVE.flush(eng)

        @block.gpsimd
        def _(eng):
            POOL.flush(eng)

        @block.tensor
        def _(eng):
            PE.flush(eng)


def kernel(**inputs):
    import concourse.bacc as bacc
    from concourse.bass_utils import run_bass_kernel_spmd

    a = {name: np.asarray(v) for name, v in inputs.items()}
    x = a["L0_attn_x"]
    B, T, D = x.shape
    rows = x.reshape(B * T, D)
    decay = np.repeat(a["L0_attn_decay_param"], D // HEADS).reshape(D // P, P).T
    arrays = {
        "x": rows, "x_t": rows.T, "w_qkv": a["L0_attn_w_qkv"], "w_out": a["L0_attn_w_out"],
        "decay_param": decay, "gate_t": a["L0_ffn_gate_w"].T,
        "w_gu": a["L0_ffn_gate_up_proj"], "w_down": a["L0_ffn_down_proj"],
        "sg_t": a["L0_ffn_shared_gate_w"].T, "su_t": a["L0_ffn_shared_up_w"].T, "sd_t": a["L0_ffn_shared_down_w"].T,
    }
    arrays = {name: np.ascontiguousarray(v) for name, v in arrays.items()}
    nc = bacc.Bacc("TRN2", target_bir_lowering=False, num_devices=1)
    aps = {name: nc.dram_tensor(name, v.shape, mybir.dt.from_np(v.dtype), kind="ExternalInput").ap()
           for name, v in arrays.items()}
    out = nc.dram_tensor("out", (B * T, D), F32, kind="ExternalOutput").ap()
    build(nc, out=out, **aps)
    r = run_bass_kernel_spmd(nc, [arrays], core_ids=[0])
    return r.results[0]["out"].reshape(B, T, D)
```
